# Optimizing a Trainium2 kernel written in Bass

```python
import numpy as np
import jax
import jax.numpy as jnp

def _softmax(x, axis=-1):
    return jax.nn.softmax(x, axis=axis)
def _gelu(x):
    return jax.nn.gelu(x, approximate=True)
def _silu(x):
    return jax.nn.silu(x)
def _sigmoid(x):
    return jax.nn.sigmoid(x)
def _layernorm(x, axis=-1, eps=1e-5):
    m = jnp.mean(x, axis=axis, keepdims=True)
    v = jnp.var(x, axis=axis, keepdims=True)
    return (x - m) / jnp.sqrt(v + eps)
def _scatter_add(tgt, idx, src, axis=0):
    return tgt.at[idx].add(src)
def _segment_sum(src, seg, n):
    return jax.ops.segment_sum(src, seg, n)

kernel_name = 'mk_adj_preln_d2_adj_64_ef8805'

def setup_inputs(seed: int = 0):
    np.random.seed(seed)
    _w = jnp.asarray
    def _rec_inputs():
        import jax
        import jax.numpy as jnp
        _gk = jax.random.key(seed)
        x = -9.806e-05 + 1 * jax.random.normal(jax.random.fold_in(_gk, 1), (4096, 64), jnp.float32)
        _a = jax.random.bernoulli(jax.random.fold_in(_gk, 2), 0.000976562, (4096, 4096))
        _a = jnp.logical_or(_a, jnp.swapaxes(_a, -1, -2))
        _a = jnp.logical_or(_a, jnp.eye(4096, dtype=bool))
        _af = _a.astype(jnp.float32)
        _af = _af * jax.random.uniform(jax.random.fold_in(_gk, 3), (4096, 4096), jnp.float32, 0.05, 5.41998)
        adj = _af
        return x, adj
    x, adj = _rec_inputs()
    def _L0_gnn_setup():
        import jax, jax.numpy as jnp
        import numpy as np
        N = 8192
        H = 64
        ALPHA = 0.2
        NEG_INF = -9000000000000000.0

        def gru_cell(x, h, w_ih, w_hh, b_ih, b_hh):
            gi = x @ w_ih.T + b_ih
            gh = h @ w_hh.T + b_hh
            ir, iz, inn = jnp.split(gi, 3, axis=1)
            hr, hz, hn = jnp.split(gh, 3, axis=1)
            r = jax.nn.sigmoid(ir + hr)
            z = jax.nn.sigmoid(iz + hz)
            n = jnp.tanh(inn + r * hn)
            return (1.0 - z) * n + z * h

        def gat(h, node_adj, edge_adj, W, a):
            hw = h @ W
            h_plus = (node_adj > 0).astype(hw.dtype) @ hw
            h_minus = (node_adj < 0).astype(hw.dtype) @ hw
            e_plus = jax.nn.leaky_relu(jnp.concatenate([h_plus, h_minus], axis=1) @ a, ALPHA)
            e_minus = jax.nn.leaky_relu(jnp.concatenate([h_minus, h_plus], axis=1) @ a, ALPHA)
            att = jnp.where(edge_adj > 0, e_plus, NEG_INF)
            att = jnp.where(edge_adj < 0, e_minus, att)
            att = jax.nn.softmax(att, axis=1)
            return att * edge_adj @ hw
        key = jax.random.key(seed)
        ks = jax.random.split(key, 12)
        f32 = jnp.float32
        inp = {'h': jax.random.normal(ks[0], (N, H), f32), 'node_adj': jax.random.normal(ks[1], (N, N), f32), 'edge_adj': jax.random.normal(ks[2], (N, N), f32), 'W_gat': jax.random.normal(ks[3], (H, H), f32) * (1.414 * np.sqrt(6.0 / (2 * H))), 'a_gat': jax.random.normal(ks[4], (2 * H, 1), f32) * (1.414 * np.sqrt(6.0 / (2 * H + 1))), 'w_ih_e': jax.random.normal(ks[5], (3 * H, 2 * H), f32) * 0.01, 'w_hh_e': jax.random.normal(ks[6], (3 * H, H), f32) * 0.01, 'b_ih_e': jnp.zeros((3 * H,), f32), 'b_hh_e': jnp.zeros((3 * H,), f32), 'w_ih_n': jax.random.normal(ks[7], (3 * H, H), f32) * 0.01, 'w_hh_n': jax.random.normal(ks[8], (3 * H, H), f32) * 0.01, 'b_ih_n': jnp.zeros((3 * H,), f32), 'b_hh_n': jnp.zeros((3 * H,), f32)}
        return inp
    _L0_gnn_all = _L0_gnn_setup()
    _L0_gnn_in = {k: v for k, v in _L0_gnn_all.items() if k in ('W_gat', 'a_gat', 'w_ih_e', 'w_hh_e', 'b_ih_e', 'b_hh_e', 'w_ih_n', 'w_hh_n', 'b_ih_n', 'b_hh_n', )}
    del _L0_gnn_all

    def _L1_gnn_setup():
        import jax, jax.numpy as jnp
        import numpy as np
        N, D_IN, D_OUT = (8192, 64, 64)
        MAX_NEIGH = 100
        DECAY = 0.5
        key = jax.random.key(seed)
        k1, k2, k3, k4 = jax.random.split(key, 4)
        stdv = 1.0 / np.sqrt(D_OUT)
        inputs = {'input': jax.random.normal(k1, (N, D_IN), dtype=jnp.float32), 'adj': jax.random.randint(k2, (N, N), 0, 2).astype(jnp.float32), 'weight': jax.random.uniform(k3, (D_IN, D_OUT), minval=-stdv, maxval=stdv, dtype=jnp.float32), 'bias': jax.random.uniform(k4, (D_OUT,), minval=-stdv, maxval=stdv, dtype=jnp.float32)}
        return inputs
    _L1_gnn_all = _L1_gnn_setup()
    _L1_gnn_in = {k: v for k, v in _L1_gnn_all.items() if k in ('weight', 'bias', )}
    del _L1_gnn_all

    return {
        "x": x,
        "adj": adj,
        "L0_gnn_W_gat": _L0_gnn_in["W_gat"],
        "L0_gnn_a_gat": _L0_gnn_in["a_gat"],
        "L0_gnn_w_ih_e": _L0_gnn_in["w_ih_e"],
        "L0_gnn_w_hh_e": _L0_gnn_in["w_hh_e"],
        "L0_gnn_b_ih_e": _L0_gnn_in["b_ih_e"],
        "L0_gnn_b_hh_e": _L0_gnn_in["b_hh_e"],
        "L0_gnn_w_ih_n": _L0_gnn_in["w_ih_n"],
        "L0_gnn_w_hh_n": _L0_gnn_in["w_hh_n"],
        "L0_gnn_b_ih_n": _L0_gnn_in["b_ih_n"],
        "L0_gnn_b_hh_n": _L0_gnn_in["b_hh_n"],
        "L1_gnn_weight": _L1_gnn_in["weight"],
        "L1_gnn_bias": _L1_gnn_in["bias"],
    }

def reference(x, adj, L0_gnn_W_gat, L0_gnn_a_gat, L0_gnn_w_ih_e, L0_gnn_w_hh_e, L0_gnn_b_ih_e, L0_gnn_b_hh_e, L0_gnn_w_ih_n, L0_gnn_w_hh_n, L0_gnn_b_ih_n, L0_gnn_b_hh_n, L1_gnn_weight, L1_gnn_bias):
    import jax
    import jax.numpy as jnp
    def _L0_gnn_ref(h, node_adj, edge_adj, W_gat, a_gat, w_ih_e, w_hh_e, b_ih_e, b_hh_e, w_ih_n, w_hh_n, b_ih_n, b_hh_n):
        import jax, jax.numpy as jnp
        import numpy as np
        N = 8192
        H = 64
        ALPHA = 0.2
        NEG_INF = -9000000000000000.0

        def gru_cell(x, h, w_ih, w_hh, b_ih, b_hh):
            gi = x @ w_ih.T + b_ih
            gh = h @ w_hh.T + b_hh
            ir, iz, inn = jnp.split(gi, 3, axis=1)
            hr, hz, hn = jnp.split(gh, 3, axis=1)
            r = jax.nn.sigmoid(ir + hr)
            z = jax.nn.sigmoid(iz + hz)
            n = jnp.tanh(inn + r * hn)
            return (1.0 - z) * n + z * h

        def gat(h, node_adj, edge_adj, W, a):
            hw = h @ W
            h_plus = (node_adj > 0).astype(hw.dtype) @ hw
            h_minus = (node_adj < 0).astype(hw.dtype) @ hw
            e_plus = jax.nn.leaky_relu(jnp.concatenate([h_plus, h_minus], axis=1) @ a, ALPHA)
            e_minus = jax.nn.leaky_relu(jnp.concatenate([h_minus, h_plus], axis=1) @ a, ALPHA)
            att = jnp.where(edge_adj > 0, e_plus, NEG_INF)
            att = jnp.where(edge_adj < 0, e_minus, att)
            att = jax.nn.softmax(att, axis=1)
            return att * edge_adj @ hw
        d_node = jnp.diag(node_adj)
        d_edge = jnp.diag(edge_adj)
        A_node = node_adj - jnp.diag(d_node)
        A_edge = edge_adj - jnp.diag(d_edge)
        node_support = jnp.concatenate([(A_node > 0).astype(h.dtype) @ h, (A_node < 0).astype(h.dtype) @ h], axis=1)
        edge_output = gru_cell(node_support, h, w_ih_e, w_hh_e, b_ih_e, b_hh_e)
        edge_support = gat(h, A_node, A_edge, W_gat, a_gat)
        node_output = gru_cell(edge_support, h, w_ih_n, w_hh_n, b_ih_n, b_hh_n)
        return d_edge[:, None] * edge_output + d_node[:, None] * node_output

    def _L1_gnn_ref(input, adj, weight, bias):
        import jax, jax.numpy as jnp
        import numpy as np
        N, D_IN, D_OUT = (8192, 64, 64)
        MAX_NEIGH = 100
        DECAY = 0.5
        support = input @ weight
        mask = (adj != 0).astype(support.dtype)
        rank = jnp.cumsum(mask, axis=1)
        deg = rank[:, -1:]
        k = jnp.minimum(deg, float(MAX_NEIGH))
        pos = rank - (deg - k)
        w = mask * jnp.where(pos > 0, DECAY ** (k - pos), 0.0)
        out = w @ support + bias
        return out

    h = jnp.maximum(_layernorm(x, axis=-1), 0.0)
    x = x + _L0_gnn_ref(h, adj, adj, L0_gnn_W_gat, L0_gnn_a_gat, L0_gnn_w_ih_e, L0_gnn_w_hh_e, L0_gnn_b_ih_e, L0_gnn_b_hh_e, L0_gnn_w_ih_n, L0_gnn_w_hh_n, L0_gnn_b_ih_n, L0_gnn_b_hh_n)
    h = jnp.maximum(_layernorm(x, axis=-1), 0.0)
    x = x + _L1_gnn_ref(h, adj, L1_gnn_weight, L1_gnn_bias)
    return x


_drawn_inputs = setup_inputs


def setup_inputs(seed=0):
    import zlib

    import numpy as np

    out = dict(_drawn_inputs(seed))
    spreads = {'L0_gnn_b_ih_e': (0.0, 0.1),
     'L0_gnn_b_hh_e': (0.0, 0.1),
     'L0_gnn_b_ih_n': (0.0, 0.1),
     'L0_gnn_b_hh_n': (0.0, 0.1)}
    factors = {'L0_gnn_w_hh_e': 3.065, 'L0_gnn_w_hh_n': 3.413}
    for name, (base, spread) in spreads.items():
        noise = np.random.default_rng([zlib.crc32(name.encode()), seed]).standard_normal(out[name].shape)
        drawn = base * np.exp(spread * noise) if base else spread * noise
        out[name] = jnp.asarray(drawn.astype(out[name].dtype))
    for name, factor in factors.items():
        out[name] = (out[name] * factor).astype(out[name].dtype)
    return out
```

```python
from contextlib import ExitStack

import concourse.bass as bass
from concourse import mybir

F32 = mybir.dt.float32
BF16 = mybir.dt.bfloat16
I8 = mybir.dt.int8
I16 = mybir.dt.int16
ALU = mybir.AluOpType
ACT = mybir.ActivationFunctionType
AX_X = mybir.AxisListType.X

P = 128
N = 4096
F = 64
S = N // P
Q = 4
TW = N // Q
BANK = 512
NCH = N // BANK
BC = BANK // P
RING = 2 * Q
MASKS = 4
G = 3 * F
RZ = 2 * F
IN, HN, HH = RZ, RZ + F, RZ + 2 * F
WA = HH + G
GROUPS = S // 2
ALPHA = 0.2
NEG_INF = -9.0e15
MAX_NEIGH = 100
UNIT = 128
SCALE = 2.0 ** (127 - MAX_NEIGH)
EPS = 1e-5
PARTS = 3


def graph_layers(nc, adj, adj_diag, x, WT, a2, wie, wie_neg, whe, win, whn, bie, bhe, bin_, bhn, w1, b1, out):
    with ExitStack() as ctx:
        def sb(name, shape, dt):
            return ctx.enter_context(nc.sbuf_tensor(name, shape, dt))

        def sem(name):
            return ctx.enter_context(nc.semaphore(name))

        ps = ctx.enter_context(nc.psum_tensor("ps", [P, 8, BANK], F32))
        signs = sb("signs", [P, S * N], I8)
        tiles = sb("tiles", [P, RING * TW], F32)
        counts = sb("counts", [P, N], BF16)
        xs = sb("xs", [P, S, F], F32)
        hx = sb("hx", [P, S * G], BF16)
        masks = sb("masks", [P, MASKS * TW], BF16)
        stage_f = sb("stage_f", [P, 2, F], F32)
        stage_b = sb("stage_b", [P, 2, G], BF16)
        ident = sb("ident", [P, P], F32)
        later = sb("later", [P, P], BF16)
        ones = sb("ones", [P, P], BF16)
        gru_w = sb("gru_w", [P, WA], F32)
        gate_w = sb("gate_w", [P, G], F32)
        score_w = sb("score_w", [P, 2], F32)
        wt_s = sb("wt_s", [F, F], F32)
        a2_s = sb("a2_s", [F, 2], F32)
        win_s = sb("win_s", [F, G], F32)
        w1_s = sb("w1_s", [F, F], F32)
        bias_rows = sb("bias_rows", [PARTS, WA], BF16)
        bias_n = sb("bias_n", [P, F], F32)
        bias_1 = sb("bias_1", [P, F], F32)
        diag = sb("diag", [P, S], F32)
        sign_sum = sb("sign_sum", [P, S * Q], F32)
        stat = sb("stat", [P, 21, S], F32)
        full_room = sb("full_room", [P, 1], F32)
        ones_f = sb("ones_f", [P, 1], F32)
        excess = sb("excess", [P, 3], F32)
        flag = sb("flag", [1, 1], mybir.dt.int32)
        kept_sums = nc.dram_tensor("kept_sums", (F, N), F32).ap()
        kept_counts = nc.dram_tensor("kept_counts", (P, N), BF16).ap()

        def slots(ap):
            return ap.rearrange("p (s f) -> p s f", s=S)

        def early(slot, n, dt):
            return signs[:, slot * N:slot * N + n * (2 if dt == BF16 else 4)].bitcast(dt)

        split1_flat = early(S - 3, S * G, BF16)
        split1 = slots(split1_flat)
        mask_diag_h = slots(early(S - 5, S * F, F32))
        adj_diag_h = slots(early(S - 7, S * F, F32))
        cen1 = slots(early(S - 9, S * F, F32))
        tmp1 = slots(early(S - 11, S * F, F32))
        bias_in = early(S - 12, 4 * G, F32)[0:1, :]
        bias_all = early(S - 13, WA, F32)[0:1, :]
        bias_parts = early(S - 14, PARTS * WA, BF16)[0:1, :]
        h_flat = hx[:, 0:2 * S * F].bitcast(F32)
        h = slots(h_flat)
        X1 = tiles[:, 0:N]
        Y = tiles[0:F, N:2 * N]
        Yn = tiles[F:P, N:2 * N]
        cen2 = slots(tiles[:, N:N + S * F])
        tmp2 = slots(tiles[:, N + S * F:2 * N])
        split2 = slots(hx[:, :])
        marks = tiles[:, 0:N].bitcast(BF16).rearrange("p (k n) -> p k n", k=2)
        codes = tiles[:, N:2 * N].bitcast(I16).rearrange("p (k n) -> p k n", k=2)
        WH = tiles[0:F, 0:N]
        gt = masks[:, :].bitcast(F32)
        rz = gt[:, 0:512].rearrange("p (g k f) -> p g k f", g=2, k=2)
        gp = gt[:, 512:896].rearrange("p (k f) -> p k f", k=2)
        nn = gt[:, 896:1152].rearrange("p (g k f) -> p g k f", g=2, k=2)
        dd = gt[:, 1152:1408].rearrange("p (g k f) -> p g k f", g=2, k=2)
        ss = gt[:, 1408:1536].rearrange("p (k f) -> p k f", k=2)
        AN = gt
        room = masks[:, :]
        (mean, var, dev, rstd, nz_d, neg_d, npos, has, ep, mx, en, e0, zz, pp, deg, nneg, n_zero, pm, term) = (
            stat[:, n, :] for n in range(19))
        neg_score = stat[:, 19:21, :].rearrange("p e s -> p (e s)").rearrange("p (s e) -> p s e", e=2)

        x_loaded = sem("x_loaded")
        diag_loaded = sem("diag_loaded")
        w_loaded = sem("w_loaded")
        gru_w_loaded = sem("gru_w_loaded")
        bias_loaded = sem("bias_loaded")
        bias_moved = sem("bias_moved")
        tile_loaded = [sem(f"tile_loaded{u}") for u in range(RING)]
        consts = sem("consts")
        bias_step = sem("bias_step")
        prep = sem("prep")
        deviation = sem("deviation")
        split_done = sem("split_done")
        diag_done = sem("diag_done")
        small_w = sem("small_w")
        small_w_out = sem("small_w_out")
        counts_step = sem("counts_step")
        masks_made = sem("masks_made")
        signs_kept = sem("signs_kept")
        masks_used = sem("masks_used")
        tiles_used = sem("tiles_used")
        sums_done = sem("sums_done")
        staged = sem("staged")
        moved = sem("moved")
        moved_a = sem("moved_a")
        turned = sem("turned")
        turned_out = sem("turned_out")
        scores = sem("scores")
        att = sem("att")
        att_exp = sem("att_exp")
        gru_pe = sem("gru_pe")
        gru_v = sem("gru_v")
        gru_a = sem("gru_a")
        norm2 = sem("norm2")
        split2_done = sem("split2_done")
        bias_added = sem("bias_added")
        behind = sem("behind")
        room_ready = sem("room_ready")
        marks_made = sem("marks_made")
        code_step = sem("code_step")
        codes_used = sem("codes_used")
        staged2 = sem("staged2")
        summed = sem("summed")
        wh_out = sem("wh_out")
        projected = sem("projected")
        final = sem("final")
        stored = sem("stored")
        degrees = sem("degrees")
        flag_step = sem("flag_step")
        excess_sum = sem("excess_sum")
        flag_ready = sem("flag_ready")
        att_final = sem("att_final")
        neg_saved = sem("neg_saved")
        neg_loaded = sem("neg_loaded")
        neg_v = sem("neg_v")
        neg_used = sem("neg_used")
        neg_reloaded = sem("neg_reloaded")
        neg_out = sem("neg_out")
        neg_scores = sem("neg_scores")
        mix_pe = sem("mix_pe")
        mix_v = sem("mix_v")

        bias_src = [bie, bhe, bin_, bhn]

        def load_flag(eng, name):
            reg = eng.alloc_register(name)
            eng.wait_ge(flag_ready, 1)
            eng.reg_load(reg, flag[0:1, 0:1])
            return reg

        block = ctx.enter_context(nc.Block())

        @block.sync
        def _(sp):
            sp.dma_start(xs[:, :, :], x).then_inc(x_loaded, 16)
            for u in range(RING):
                sp.dma_start(tiles[:, u * TW:(u + 1) * TW], adj[:, u * TW:(u + 1) * TW]).then_inc(tile_loaded[u], 16)
            with sp.Fori(1, S // 2) as it:
                for u in range(RING):
                    sp.wait_ge(tiles_used, it * RING + (u + 1 - RING))
                    sp.wait_ge(masks_made, it * RING + (u + 1 - RING))
                    sp.wait_ge(signs_kept, it * RING + (u + 1 - RING))
                    sp.dma_start(tiles[:, u * TW:(u + 1) * TW],
                                 adj[:, bass.ds(it * (2 * N) + u * TW, TW)]).then_inc(tile_loaded[u], 16)

            has_neg = load_flag(sp, "sp_neg")
            with sp.If_ne(has_neg, 0):
                sp.wait_ge(moved, NCH)
                sp.dma_start(kept_sums, X1[0:F, :]).then_inc(neg_saved, 16)
                sp.dma_start(kept_counts, counts[:, :]).then_inc(neg_saved, 16)
                sp.wait_ge(neg_saved, 32)
                with sp.Fori(0, S) as s:
                    sp.wait_ge(neg_used, s + 1)
                    sp.dma_start(tiles[:, 0:N], adj[:, bass.ds(s * N, N)]).then_inc(neg_loaded, 16)
                sp.wait_ge(neg_used, S + 1)
                sp.dma_start(X1[0:F, :], kept_sums).then_inc(neg_reloaded, 16)
                sp.wait_ge(neg_scores, 1)
                sp.dma_start(counts[:, :], kept_counts).then_inc(neg_reloaded, 16)

            sp.wait_ge(final, Q)
            sp.dma_start(out, xs[:, :, :]).then_inc(stored, 16)
            sp.wait_ge(stored, 16)

        @block.gpsimd
        def _(pool):
            pool.memset(ident[:, :], 1.0).then_inc(consts, 1)
            pool.memset(later[:, :], -1.0).then_inc(consts, 1)
            pool.memset(ones[:, :], 1.0).then_inc(consts, 1)
            pool.memset(full_room[:, :], float(MAX_NEIGH)).then_inc(consts, 1)
            pool.memset(gru_w[:, :], 0.0).then_inc(consts, 1)
            pool.memset(ones_f[:, :], 1.0).then_inc(consts, 1)
            pool.memset(stat[:, 15, :], 0.0).then_inc(consts, 1)
            pool.memset(stat[:, 19:21, :], 0.0).then_inc(consts, 1)
            pool.wait_ge(consts, 8)
            pool.affine_select(out=ident[:, :], in_=ident[:, :], compare_op=ALU.is_equal, fill=0.0, base=0,
                               pattern=[[-1, P]], channel_multiplier=1).then_inc(consts, 1)
            pool.affine_select(out=later[:, :], in_=later[:, :], compare_op=ALU.is_gt, fill=0.0, base=0,
                               pattern=[[-1, P]], channel_multiplier=1).then_inc(consts, 1)

            pool.wait_ge(bias_loaded, 16 * 4)
            be_i, be_h, bn_i, bn_h = (bias_in[:, n * G:(n + 1) * G] for n in range(4))
            pool.tensor_tensor(bias_all[:, 0:RZ], be_i[:, 0:RZ], be_h[:, 0:RZ], ALU.add).then_inc(bias_step, 1)
            pool.tensor_copy(bias_all[:, IN:HN], be_i[:, RZ:G]).then_inc(bias_step, 1)
            pool.tensor_copy(bias_all[:, HN:HH], be_h[:, RZ:G]).then_inc(bias_step, 1)
            pool.tensor_tensor(bias_all[:, HH:HH + RZ], bn_i[:, 0:RZ], bn_h[:, 0:RZ], ALU.add).then_inc(bias_step, 1)
            pool.tensor_copy(bias_all[:, HH + RZ:WA], bn_h[:, RZ:G]).then_inc(bias_step, 1)
            pool.wait_ge(bias_step, 5)
            for part in range(PARTS):
                piece = bias_parts[:, part * WA:(part + 1) * WA]
                pool.tensor_copy(piece, bias_all[:, :]).then_inc(bias_step, 1)
                pool.wait_ge(bias_step, 6 + 2 * part)
                if part < PARTS - 1:
                    pool.tensor_tensor(bias_all[:, :], bias_all[:, :], piece, ALU.subtract).then_inc(bias_step, 1)
                    pool.wait_ge(bias_step, 7 + 2 * part)

            def stage(it, k):
                pool.tensor_copy(stage_f[:, k, :], h_flat[:, bass.ds(it * (2 * F) + k * F, F)]).then_inc(staged, 1)
                pool.tensor_copy(stage_b[:, k, :],
                                 split1_flat[:, bass.ds(it * (2 * G) + k * G, G)]).then_inc(staged, 1)

            pool.wait_ge(split_done, 1)
            for k in range(2):
                stage(0, k)
            with pool.Fori(1, S // 2) as it:
                for k in range(2):
                    pool.wait_ge(tiles_used, it * RING + (k + 1) * Q - RING)
                    stage(it, k)

            pool.wait_ge(norm2, 4)
            pool.tensor_tensor(xs[:, :, :], xs[:, :, :], bias_1[:, None, :].to_broadcast((P, S, F)), ALU.add)\
                .then_inc(bias_added, 1)

            def stage2(it, k):
                pool.tensor_copy(stage_b[:, k, :], hx[:, bass.ds(it * (2 * G) + k * G, G)]).then_inc(staged2, 1)

            pool.wait_ge(split2_done, 1)
            for k in range(2):
                stage2(0, k)
            with pool.Fori(1, S // 2) as it:
                for k in range(2):
                    pool.wait_ge(codes_used, it * 2 + (k - 1))
                    stage2(it, k)

        @block.scalar
        def _(act):
            act.dma_start(diag[:, :], adj_diag).then_inc(diag_loaded, 16)
            for dst, src in ((wt_s, WT), (a2_s, a2), (win_s, win), (w1_s, w1)):
                act.dma_start(dst[:, :], src).then_inc(w_loaded, 16)
            for n, b in enumerate(bias_src):
                act.dma_start(bias_in[:, n * G:(n + 1) * G], b.rearrange("(a n) -> a n", a=1)).then_inc(bias_loaded, 16)
            act.dma_start(bias_n[:, :], bass.AP(tensor=bin_.tensor, offset=RZ, ap=[[0, P], [1, F]])).then_inc(w_loaded, 16)
            act.dma_start(bias_1[:, :], bass.AP(tensor=b1.tensor, offset=0, ap=[[0, P], [1, F]])).then_inc(w_loaded, 16)
            act.wait_ge(consts, 10)
            act.dma_start(gru_w[0:F, 0:G], wie).then_inc(gru_w_loaded, 16)
            act.dma_start(gru_w[F:P, 0:RZ], whe[:, 0:RZ]).then_inc(gru_w_loaded, 16)
            act.dma_start(gru_w[F:P, HN:HH], whe[:, RZ:G]).then_inc(gru_w_loaded, 16)
            act.dma_start(gru_w[F:P, HH:WA], whn).then_inc(gru_w_loaded, 16)
            act.dma_start(gate_w[F:P, :], wie_neg).then_inc(gru_w_loaded, 16)
            act.wait_ge(prep, 7)
            act.activation(dev, var, ACT.Sqrt).then_inc(deviation, 1)
            act.wait_ge(bias_step, 10)
            act.dma_start(bias_rows[:, :], bias_parts[:, :].rearrange("a (r n) -> a r n", r=PARTS))\
                .then_inc(bias_moved, 16)

            def keep_signs(it):
                for u in range(RING):
                    act.wait_ge(tile_loaded[u], it * 16 + 16)
                    if u % Q == 0:
                        act.wait_ge(staged, it * 4 + 2 + 2 * (u // Q))
                    act.activation(signs[:, bass.ds(it * (2 * N) + u * TW, TW)], tiles[:, u * TW:(u + 1) * TW],
                                   ACT.Sign, accum_out=sign_sum[:, bass.ds(it * RING + u, 1)]).then_inc(signs_kept, 1)

            keep_signs(0)
            act.wait_ge(sums_done, 1)
            act.wait_ge(bias_moved, 16)
            with act.Fori(1, S // 2) as it:
                keep_signs(it)

            act.wait_ge(tiles_used, S * Q)
            act.wait_ge(masks_made, S * Q)
            act.wait_ge(signs_kept, S * Q)
            for c in (2, 3, 4, 5, 6, 7, 0, 1):
                k = F * (c % 2)
                act.activation(Y[:, c * BANK:(c + 1) * BANK], ps[k:k + F, Q + c // 2, :], ACT.Copy).then_inc(moved_a, 1)
            for c in range(NCH):
                act.wait_ge(turned, c + 1)
                act.activation(X1[F:P, c * BANK:(c + 1) * BANK], ps[F:P, 6 + c % 2, :], ACT.Copy)\
                    .then_inc(turned_out, 1)

            for e in (ep, en, e0):
                act.wait_ge(att, ATT_EXP)
                act.activation(e, e, ACT.Exp).then_inc(att_exp, 1)

            def gru(it, first):
                for k in range(2):
                    A = ps[:, 3 * k:3 * k + 2, :]
                    B = ps[:, 3 * k + 2, :].rearrange("p (b n) -> p b n", n=G + F)
                    act.wait_ge(gru_pe, it * 2 + k + 1)
                    if not (first and k == 0):
                        act.wait_ge(gru_v, it * (2 * GV) + k * GV)
                    else:
                        act.wait_ge(att_final, 1)
                    act.activation(rz[:, 0, :, :], A[:, :, 0:RZ], ACT.Sigmoid).then_inc(gru_a, 1)
                    for b in range(2):
                        act.activation(gp[:, b, :], B[:, b, 0:G], ACT.Copy,
                                       scale=pp[:, bass.ds(it * 4 + 2 * k + b, 1)]).then_inc(gru_a, 1)
                    act.wait_ge(gru_v, it * (2 * GV) + k * GV + 1)
                    act.activation(rz[:, 1, :, :], rz[:, 1, :, :], ACT.Sigmoid).then_inc(gru_a, 1)
                    act.wait_ge(gru_v, it * (2 * GV) + k * GV + 7)
                    act.activation(nn[:, :, :, :], nn[:, :, :, :], ACT.Tanh).then_inc(gru_a, 1)

            gru(0, True)
            with act.Fori(1, GROUPS // 2) as it:
                gru(it, False)

            act.wait_ge(norm2, 7)
            act.activation(dev, var, ACT.Sqrt).then_inc(deviation, 1)
            for c in range(NCH):
                act.wait_ge(behind, c + 1)
                act.activation(room[:, c * BANK:(c + 1) * BANK], ps[:, Q + c % Q, :], ACT.Relu,
                               bias=full_room[:, :]).then_inc(room_ready, 1)

            def mark(it, first):
                for k in range(2):
                    if not first:
                        act.wait_ge(code_step, it * 6 + 3 * k - 4)
                    act.activation(marks[:, k, :], signs[:, bass.ds(it * (2 * N) + k * N, N)], ACT.Abs)\
                        .then_inc(marks_made, 1)

            mark(0, True)
            with act.Fori(1, S // 2) as it:
                mark(it, False)
            act.wait_ge(summed, 1)
            for c in range(0, NCH, 2):
                act.activation(WH[:, c * BANK:(c + 1) * BANK], ps[0:F, c // 2, :], ACT.Copy).then_inc(wh_out, 1)

        @block.vector
        def _(dve):
            def link(ins, s, n=[0], seen={}):
                seen[s.name] = seen.get(s.name, 0) + 1
                ins.then_inc(s, 1)
                dve.wait_ge(s, seen[s.name])
                return seen[s.name]

            def bc(v):
                return v[:, :, None].to_broadcast((P, S, F))

            def normalise(src, cen, tmp, dst, scale, s, n_dev):
                link(dve.tensor_reduce(mean, src, AX_X, ALU.add), s)
                link(dve.tensor_scalar(mean, mean, 1.0 / F, None, ALU.mult), s)
                link(dve.tensor_tensor(cen, src, bc(mean), ALU.subtract), s)
                link(dve.tensor_tensor(tmp, cen, cen, ALU.mult), s)
                link(dve.tensor_reduce(var, tmp, AX_X, ALU.add), s)
                link(dve.tensor_scalar(var, var, 1.0 / F, EPS, ALU.mult, ALU.add), s)
                dve.wait_ge(deviation, n_dev)
                link(dve.reciprocal(rstd, dev), s)
                if scale != 1.0:
                    link(dve.tensor_scalar(rstd, rstd, scale, None, ALU.mult), s)
                link(dve.scalar_tensor_tensor(out=dst, in0=cen, scalar=0.0, in1=bc(rstd), op0=ALU.max,
                                              op1=ALU.mult), s)

            def split(src, rest, parts, s, done):
                link(dve.tensor_copy(parts[:, :, 0:F], src), s)
                link(dve.tensor_tensor(rest, src, parts[:, :, 0:F], ALU.subtract), s)
                link(dve.tensor_copy(parts[:, :, F:2 * F], rest), s)
                dve.tensor_tensor(parts[:, :, 2 * F:G], rest, parts[:, :, F:2 * F], ALU.subtract).then_inc(done, 1)

            link(dve.memset(counts[:, :], 0.0), prep)
            dve.wait_ge(x_loaded, 16)
            normalise(xs[:, :, :], cen1, tmp1, h, 1.0, prep, 1)
            split(h, tmp1, split1, prep, split_done)
            dve.wait_ge(diag_loaded, 16)
            link(dve.tensor_scalar(nz_d, diag[:, :], 0.0, -1.0, ALU.not_equal, ALU.mult), prep)
            link(dve.tensor_scalar(neg_d, diag[:, :], -1.0, None, ALU.mult), prep)
            dve.tensor_tensor(mask_diag_h, h, bc(nz_d), ALU.mult).then_inc(diag_done, 1)
            dve.tensor_tensor(adj_diag_h, h, bc(neg_d), ALU.mult).then_inc(diag_done, 1)
            dve.wait_ge(small_w, 1)
            dve.tensor_copy(gate_w[0:F, :], ps[0:F, 7, 0:G]).then_inc(small_w_out, 1)
            for k in (0, F):
                dve.tensor_copy(score_w[k:k + F, :], ps[0:F, 7, G:G + 2]).then_inc(small_w_out, 1)

            def make_masks(it, first):
                for u in range(0, RING, 2):
                    for v in (u, u + 1):
                        dve.wait_ge(tile_loaded[v], it * 16 + 16)
                        if not (first and v < MASKS):
                            dve.wait_ge(masks_used, it * RING + (v + 1 - MASKS))
                            dve.wait_ge(counts_step, it * RING + (v + 1 - MASKS))
                        dve.tensor_scalar(masks[:, (v % MASKS) * TW:(v % MASKS + 1) * TW],
                                          tiles[:, v * TW:(v + 1) * TW], 0.0, None, ALU.not_equal)\
                            .then_inc(masks_made, 1)
                    for v in (u, u + 1):
                        dve.wait_ge(masks_made, it * RING + (v + 1))
                        if not (first and v < Q):
                            dve.wait_ge(counts_step, it * RING + (v + 1 - Q))
                        part = counts[:, (v % Q) * TW:(v % Q + 1) * TW]
                        dve.tensor_tensor(part, part, masks[:, (v % MASKS) * TW:(v % MASKS + 1) * TW], ALU.add)\
                            .then_inc(counts_step, 1)

            make_masks(0, True)
            with dve.Fori(1, S // 2) as it:
                make_masks(it, False)

            dve.wait_ge(tiles_used, S * Q)
            dve.wait_ge(masks_made, S * Q)
            dve.wait_ge(signs_kept, S * Q)
            for c in range(NCH):
                k = F * (c % 2)
                dve.tensor_copy(X1[0:F, c * BANK:(c + 1) * BANK], ps[k:k + F, c // 2, :]).then_inc(moved, 1)

            dve.wait_ge(degrees, 1)
            dve.wait_ge(consts, 10)
            link(dve.tensor_copy(deg, ps[:, 5, 2 * S:3 * S]), flag_step)
            link(dve.tensor_reduce(excess[:, 0:1], deg, AX_X, ALU.add), flag_step)
            link(dve.tensor_reduce(excess[:, 1:2], sign_sum[:, :], AX_X, ALU.add), flag_step)
            link(dve.tensor_tensor(excess[:, 2:3], excess[:, 0:1], excess[:, 1:2], ALU.subtract), flag_step)
            dve.wait_ge(excess_sum, 1)
            dve.tensor_copy(flag[:, :], ps[0:1, 5, 0:1]).then_inc(flag_ready, 1)

            has_neg = load_flag(dve, "dve_neg")
            with dve.If_ne(has_neg, 0):
                dve.wait_ge(neg_saved, 32)
                dve.memset(counts[:, :], 0.0).then_inc(neg_v, 1)
                dve.wait_ge(neg_v, 1)
                with dve.Fori(0, S) as s:
                    dve.wait_ge(neg_loaded, s * 16 + 16)
                    dve.wait_ge(neg_used, s + 1)
                    hs = h_flat[:, bass.ds(s * F, F)]
                    own = tiles[:, bass.ds(s * P, P)]
                    dve.tensor_scalar(stage_f[:, 0, :], hs, 1.0, None, ALU.mult).then_inc(neg_v, 1)
                    dve.tensor_scalar(stage_b[:, 0, 0:F], hs, 1.0, None, ALU.mult).then_inc(neg_v, 1)
                    dve.scalar_tensor_tensor(out=own, in0=ident[:, :], scalar=0.0, in1=own, op0=ALU.is_equal,
                                             op1=ALU.mult).then_inc(neg_v, 1)
                    dve.wait_ge(neg_v, s * 9 + 4)
                    dve.tensor_tensor(stage_f[:, 1, :], stage_f[:, 0, :], stage_b[:, 0, 0:F], ALU.subtract)\
                        .then_inc(neg_v, 1)
                    dve.wait_ge(neg_v, s * 9 + 5)
                    dve.tensor_scalar(stage_b[:, 0, F:2 * F], stage_f[:, 1, :], 1.0, None, ALU.mult).then_inc(neg_v, 1)
                    dve.wait_ge(neg_v, s * 9 + 6)
                    dve.tensor_tensor(stage_b[:, 0, 2 * F:G], stage_f[:, 1, :], stage_b[:, 0, F:2 * F], ALU.subtract)\
                        .then_inc(neg_v, 1)
                    dve.tensor_scalar(masks[:, :], tiles[:, 0:N], 0.0, None, ALU.is_lt).then_inc(neg_v, 1)
                    dve.wait_ge(neg_v, s * 9 + 8)
                    dve.tensor_scalar(tiles[:, 0:N], tiles[:, 0:N], 0.0, None, ALU.min).then_inc(neg_v, 1)
                    dve.tensor_tensor(counts[:, :], counts[:, :], masks[:, :], ALU.add).then_inc(neg_v, 1)
                    dve.wait_ge(neg_v, s * 9 + 10)
                dve.wait_ge(neg_used, S + 1)
                dve.wait_ge(neg_reloaded, 16)
                dve.wait_ge(moved_a, NCH)
                for c in range(NCH):
                    k = F * (c % 2)
                    at = slice(c * BANK, (c + 1) * BANK)
                    dve.tensor_copy(Yn[:, at], ps[k:k + F, c // 2, :]).then_inc(neg_out, 1)
                    dve.tensor_tensor(X1[0:F, at], X1[0:F, at], ps[k:k + F, c // 2, :], ALU.subtract).then_inc(neg_out, 1)
                    dve.tensor_tensor(Y[:, at], Y[:, at], ps[k:k + F, Q + c // 2, :], ALU.subtract).then_inc(neg_out, 1)
                dve.tensor_copy(AN, ps[:, Q:2 * Q, :].rearrange("p b n -> p (b n)")).then_inc(neg_out, 1)
                dve.wait_ge(neg_out, 3 * NCH + 1)
                dve.wait_ge(neg_scores, 1)
                dve.tensor_copy(neg_score, ps[:, 5, 3 * S:5 * S].rearrange("p (s e) -> p s e", e=2)).then_inc(neg_out, 1)
                dve.tensor_copy(nneg, ps[:, 5, 5 * S:6 * S]).then_inc(neg_out, 1)
                dve.wait_ge(neg_out, 3 * NCH + 3)

            dve.wait_ge(scores, 1)
            E = ps[:, 5, 0:2 * S].rearrange("p (s e) -> p s e", e=2)
            link(dve.tensor_tensor(npos, deg, nz_d, ALU.add), att)
            link(dve.tensor_scalar(n_zero, npos, -1.0, float(N), ALU.mult, ALU.add), att)
            link(dve.tensor_tensor(npos, npos, nneg, ALU.subtract), att)
            for e, own, other, many in ((ep, 0, 1, npos), (en, 1, 0, nneg)):
                link(dve.tensor_tensor(e, E[:, :, own], neg_score[:, :, other], ALU.add), att)
                link(dve.tensor_scalar(term, e, ALPHA, None, ALU.mult), att)
                link(dve.tensor_tensor(e, e, term, ALU.max), att)
                link(dve.tensor_scalar(has, many, 0.5, None, ALU.is_ge), att)
                link(dve.tensor_tensor(e, e, has, ALU.mult), att)
                link(dve.tensor_scalar(has, has, 1.0, -NEG_INF, ALU.subtract, ALU.mult), att)
                link(dve.tensor_tensor(e, e, has, ALU.add), att)
            link(dve.tensor_tensor(mx, ep, en, ALU.max), att)
            link(dve.tensor_scalar(mx, mx, NEG_INF, None, ALU.max), att)
            link(dve.tensor_tensor(ep, ep, mx, ALU.subtract), att)
            link(dve.tensor_tensor(en, en, mx, ALU.subtract), att)
            n = link(dve.tensor_scalar(e0, mx, -1.0, NEG_INF, ALU.mult, ALU.add), att)
            assert n == ATT_EXP
            dve.wait_ge(att_exp, 3)
            link(dve.tensor_tensor(zz, ep, npos, ALU.mult), att)
            link(dve.tensor_tensor(term, en, nneg, ALU.mult), att)
            link(dve.tensor_tensor(zz, zz, term, ALU.add), att)
            link(dve.tensor_tensor(e0, e0, n_zero, ALU.mult), att)
            link(dve.tensor_tensor(zz, zz, e0, ALU.add), att)
            link(dve.reciprocal(zz, zz), att)
            link(dve.tensor_tensor(pp, ep, zz, ALU.mult), att)
            link(dve.tensor_tensor(pm, en, zz, ALU.mult), att)

            with dve.If_ne(has_neg, 0):
                with dve.Fori(0, Q) as it:
                    for j in range(2):
                        k = F * j
                        for b in range(BC):
                            dve.wait_ge(mix_pe, it * (2 * BC) + (j * BC + b + 1))
                            for n, w in enumerate((pp, pm)):
                                one = w[:, bass.ds(it * (2 * BC) + j * BC + b, 1)]
                                dve.tensor_copy(stage_f[:, n, :], one.to_broadcast((P, F))).then_inc(mix_v, 1)
                        base = it * 22 + 11 * j
                        dve.wait_ge(mix_pe, it * (2 * BC) + (j * BC + BC + 1))
                        Yc = Y[:, bass.ds(it * (2 * BANK) + j * BANK, BANK)]
                        dve.tensor_tensor(Yc, Yc, ps[0:F, 0, :], ALU.mult).then_inc(mix_v, 1)
                        dve.tensor_tensor(ps[0:F, 2, :], AN[k:k + F, bass.ds(it * BANK, BANK)], ps[k:k + F, 1, :],
                                          ALU.mult).then_inc(mix_v, 1)
                        dve.wait_ge(mix_v, base + 10)
                        dve.tensor_tensor(Yc, Yc, ps[0:F, 2, :], ALU.add).then_inc(mix_v, 1)
                dve.memset(pp, 1.0).then_inc(mix_v, 1)
                dve.wait_ge(mix_v, Q * 22 + 1)
            dve.nop().then_inc(att_final, 1)

            def gru(it, first):
                for k in range(2):
                    A = ps[:, 3 * k:3 * k + 2, :]
                    hk = h[:, bass.ds(it * 4 + 2 * k, 2), :]
                    step = [it * (2 * GV) + k * GV]

                    def then(ins):
                        ins.then_inc(gru_v, 1)
                        step[0] = step[0] + 1

                    def done():
                        dve.wait_ge(gru_v, step[0])

                    base_a = it * 10 + 5 * k
                    dve.wait_ge(gru_pe, it * 2 + k + 1)
                    dve.wait_ge(gru_a, base_a + 3)
                    then(dve.tensor_tensor(rz[:, 1, :, :], gp[:, :, 0:RZ], A[:, :, HH:HH + RZ], ALU.add))
                    then(dve.tensor_tensor(nn[:, 0, :, :], rz[:, 0, :, 0:F], A[:, :, HN:HH], ALU.mult))
                    done()
                    then(dve.tensor_tensor(nn[:, 0, :, :], nn[:, 0, :, :], A[:, :, IN:HN], ALU.add))
                    then(dve.tensor_tensor(gp[:, :, RZ:G], gp[:, :, RZ:G],
                                           bias_n[:, None, :].to_broadcast((P, 2, F)), ALU.add))
                    dve.wait_ge(gru_a, base_a + 4)
                    then(dve.tensor_tensor(nn[:, 1, :, :], rz[:, 1, :, 0:F], A[:, :, HH + RZ:WA], ALU.mult))
                    done()
                    then(dve.tensor_tensor(nn[:, 1, :, :], nn[:, 1, :, :], gp[:, :, RZ:G], ALU.add))
                    then(dve.tensor_copy(ss[:, :, :], hk))
                    done()
                    dve.wait_ge(gru_a, base_a + 5)
                    then(dve.tensor_tensor(dd[:, :, :, :], hk[:, None, :, :].to_broadcast((P, 2, 2, F)),
                                           nn[:, :, :, :], ALU.subtract))
                    done()
                    then(dve.tensor_tensor(dd[:, :, :, :], dd[:, :, :, :], rz[:, :, :, F:RZ], ALU.mult))
                    done()
                    then(dve.tensor_tensor(dd[:, :, :, :], dd[:, :, :, :], nn[:, :, :, :], ALU.add))
                    done()
                    then(dve.tensor_tensor(ss[:, :, :], dd[:, 0, :, :], dd[:, 1, :, :], ALU.add))
                    done()
                    for b in range(2):
                        xk = xs[:, bass.ds(it * 4 + 2 * k + b, 1), :]
                        then(dve.scalar_tensor_tensor(out=xk, in0=ss[:, b:b + 1, :],
                                                      scalar=diag[:, bass.ds(it * 4 + 2 * k + b, 1)],
                                                      in1=xk, op0=ALU.mult, op1=ALU.add))

            gru(0, True)
            with dve.Fori(1, GROUPS // 2) as it:
                gru(it, False)
            dve.wait_ge(gru_v, GROUPS * GV)

            link(dve.memset(mean, 0.0), norm2)
            normalise(xs[:, :, :], cen2, tmp2, tmp2, SCALE, norm2, 2)
            split(tmp2, cen2, split2, norm2, split2_done)

            def encode(it, first):
                for k in range(2):
                    base = it * 6 + 3 * k
                    dve.wait_ge(marks_made, it * 2 + (k + 1))
                    if not first:
                        dve.wait_ge(codes_used, it * 2 + (k - 1))
                    if not (first and k == 0):
                        dve.wait_ge(code_step, base)
                    dve.tensor_tensor(codes[:, k, :], marks[:, k, :], room, ALU.mult).then_inc(code_step, 1)
                    dve.wait_ge(code_step, base + 1)
                    dve.tensor_tensor(room, room, marks[:, k, :], ALU.subtract).then_inc(code_step, 1)
                    dve.tensor_scalar(codes[:, k, :], codes[:, k, :], 0.0, float(UNIT), ALU.max, ALU.mult)\
                        .then_inc(code_step, 1)

            dve.wait_ge(split2_done, 1)
            dve.wait_ge(room_ready, NCH)
            encode(0, True)
            with dve.Fori(1, S // 2) as it:
                encode(it, False)

            dve.wait_ge(summed, 1)
            for c in range(1, NCH, 2):
                dve.tensor_copy(WH[:, c * BANK:(c + 1) * BANK], ps[F:P, c // 2, :]).then_inc(wh_out, 1)
            dve.wait_ge(bias_added, 1)
            for q in range(Q):
                dve.wait_ge(projected, q + 1)
                xq = xs[:, q * (S // Q):(q + 1) * (S // Q), :]
                dve.tensor_tensor(xq, ps[:, Q + q, :].rearrange("p (s f) -> p s f", f=F), xq, ALU.add)\
                    .then_inc(final, 1)

        @block.tensor
        def _(pe):
            def mm(dst, lhsT, rhs, start=False, stop=False):
                return pe.matmul(dst, lhsT, rhs, start=start, stop=stop, skip_group_check=True)

            pe.wait_ge(w_loaded, 16 * 6)
            mm(ps[0:F, 7, 0:G], wt_s[:, :], win_s[:, :], True, True)
            mm(ps[0:F, 7, G:G + 2], wt_s[:, :], a2_s[:, :], True, True).then_inc(small_w, 1)
            pe.wait_ge(small_w_out, 3)
            pe.wait_ge(consts, 10)

            def products(it, first):
                for u in range(RING):
                    k, q = divmod(u, Q)
                    if q == 0:
                        pe.wait_ge(staged, it * 4 + 2 * k + 2)
                    begin = first and k == 0
                    pe.wait_ge(masks_made, it * RING + (u + 1))
                    m = masks[:, (u % MASKS) * TW:(u % MASKS + 1) * TW]
                    for part in range(PARTS):
                        for c in range(2):
                            last = mm(ps[c * F:(c + 1) * F, q, :], stage_b[:, k, part * F:(part + 1) * F],
                                      m[:, c * BANK:(c + 1) * BANK], begin and part == 0)
                    last.then_inc(masks_used, 1)
                    pe.wait_ge(tile_loaded[u], it * 16 + 16)
                    for c in range(2):
                        last = mm(ps[c * F:(c + 1) * F, Q + q, :], stage_f[:, k, :],
                                  tiles[:, u * TW + c * BANK:u * TW + (c + 1) * BANK], begin)
                    last.then_inc(tiles_used, 1)

            products(0, True)
            pe.wait_ge(diag_done, 2)
            for s in range(S):
                c, b = divmod(s, BC)
                k = F * (c % 2)
                mm(ps[k:k + F, c // 2, b * P:(b + 1) * P], mask_diag_h[:, s, :], ident[:, :])
                last = mm(ps[k:k + F, Q + c // 2, b * P:(b + 1) * P], adj_diag_h[:, s, :], ident[:, :])
            last.then_inc(sums_done, 1)
            with pe.Fori(1, S // 2) as it:
                products(it, False)

            pe.wait_ge(moved_a, 2)
            pe.wait_ge(counts_step, S * Q)
            for s in range(S):
                last = mm(ps[:, 5, 2 * S + s:2 * S + s + 1], counts[:, s * P:(s + 1) * P], ones[:, 0:1], True, True)
            last.then_inc(degrees, 1)
            pe.wait_ge(flag_step, 4)
            mm(ps[0:1, 5, 0:1], excess[:, 2:3], ones_f[:, :], True, True).then_inc(excess_sum, 1)

            def negative_products(s, first):
                pe.wait_ge(neg_v, s * 9 + 10)
                for q in range(Q):
                    for part in range(PARTS):
                        for c in range(2):
                            at = (2 * q + c) * BANK
                            mm(ps[c * F:(c + 1) * F, q, :], stage_b[:, 0, part * F:(part + 1) * F],
                               masks[:, at:at + BANK], first and part == 0)
                    for c in range(2):
                        at = (2 * q + c) * BANK
                        last = mm(ps[c * F:(c + 1) * F, Q + q, :], stage_f[:, 0, :], tiles[:, at:at + BANK], first)
                last.then_inc(neg_used, 1)

            has_neg = load_flag(pe, "pe_neg")
            with pe.If_ne(has_neg, 0):
                pe.wait_ge(moved, NCH)
                pe.wait_ge(moved_a, NCH)
                pe.nop().then_inc(neg_used, 1)
                negative_products(0, True)
                with pe.Fori(1, S) as s:
                    negative_products(s, False)
                pe.wait_ge(neg_out, 3 * NCH + 1)
                for s in range(S):
                    mm(ps[:, 5, 3 * S + 2 * s:3 * S + 2 * s + 2], Yn[:, s * P:(s + 1) * P], score_w[F:P, :], True, True)
                    last = mm(ps[:, 5, 5 * S + s:5 * S + s + 1], counts[:, s * P:(s + 1) * P], ones[:, 0:1], True, True)
                last.then_inc(neg_scores, 1)
                pe.wait_ge(neg_reloaded, 32)
                pe.wait_ge(neg_out, 3 * NCH + 3)

            pe.wait_ge(moved, NCH)
            for s in range(S):
                last = mm(ps[:, 5, 2 * s:2 * s + 2], X1[0:F, s * P:(s + 1) * P], score_w[0:F, :], True, True)
            last.then_inc(scores, 1)
            pe.wait_ge(moved_a, NCH)
            for c in range(NCH):
                if c >= 2:
                    pe.wait_ge(turned_out, c - 1)
                for b in range(BC):
                    last = mm(ps[F:P, 6 + c % 2, b * P:(b + 1) * P], h[:, c * BC + b, :], ident[:, :], True, True)
                last.then_inc(turned, 1)

            with pe.If_ne(has_neg, 0):
                pe.nop().then_inc(mix_pe, 1)
                with pe.Fori(0, Q) as it:
                    for j in range(2):
                        for b in range(BC):
                            pe.wait_ge(mix_v, it * 22 + (11 * j + 2 * b + 2))
                            mm(ps[0:F, 0, b * P:(b + 1) * P], stage_f[:, 0, :], ident[:, :], True, True)
                            mm(ps[j * F:(j + 1) * F, 1, b * P:(b + 1) * P], stage_f[:, 1, :], ident[:, :], True, True)\
                                .then_inc(mix_pe, 1)
                pe.wait_ge(mix_v, Q * 22 + 1)

            pe.wait_ge(bias_moved, 16)
            pe.wait_ge(gru_w_loaded, 16 * 5)
            pe.wait_ge(turned_out, NCH)
            pe.wait_ge(moved_a, NCH)
            for g in range(GROUPS):
                k = g % 2
                if g == 1:
                    pe.wait_ge(att_final, 1)
                if g >= 2:
                    pe.wait_ge(gru_v, (g - 2) * GV + 5)
                for b in range(2):
                    s = 2 * g + b
                    bank = ps[:, 3 * k + b, 0:WA]
                    mm(bank, ones[0:PARTS, :], bias_rows[:, :], True)
                    with pe.If_ne(has_neg, 0):
                        mm(ps[:, 3 * k + b, 0:G], Yn[:, s * P:(s + 1) * P], gate_w[F:P, :])
                    mm(bank, X1[:, s * P:(s + 1) * P], gru_w[:, :], False, True)
                    last = mm(ps[:, 3 * k + 2, b * (G + F):b * (G + F) + G], Y[:, s * P:(s + 1) * P], gate_w[0:F, :],
                              True, True)
                last.then_inc(gru_pe, 1)

            pe.wait_ge(gru_v, GROUPS * GV)
            for c in range(NCH):
                if c >= Q:
                    pe.wait_ge(room_ready, c - Q + 1)
                mm(ps[:, Q + c % Q, :], later[:, :], counts[:, c * BANK:(c + 1) * BANK], True, True).then_inc(behind, 1)

            def decayed(it, first):
                for k in range(2):
                    pe.wait_ge(staged2, it * 2 + (k + 1))
                    pe.wait_ge(code_step, it * 6 + (3 * k + 3))
                    for q in range(Q):
                        for part in range(PARTS):
                            for c in range(2):
                                at = (2 * q + c) * BANK
                                last = mm(ps[c * F:(c + 1) * F, q, :], stage_b[:, k, part * F:(part + 1) * F],
                                          codes[:, k, at:at + BANK].bitcast(BF16), first and k == 0 and part == 0)
                    last.then_inc(codes_used, 1)

            decayed(0, True)
            with pe.Fori(1, S // 2 - 1) as it:
                decayed(it, False)
            decayed(S // 2 - 1, False)
            pe.wait_ge(codes_used, S)
            pe.nop().then_inc(summed, 1)
            for q in range(Q):
                pe.wait_ge(wh_out, NCH)
                for b in range(S // Q):
                    s = q * (S // Q) + b
                    last = mm(ps[:, Q + q, b * F:(b + 1) * F], WH[:, s * P:(s + 1) * P], w1_s[:, :], True, True)
                last.then_inc(projected, 1)


GV = 13
ATT_EXP = 22


_ORDER = ["adj", "adj_diag", "x", "WT", "a2", "wie", "wie_neg", "whe", "win", "whn", "bie", "bhe", "bin", "bhn", "w1", "b1"]


def kernel(**inputs):
    import numpy as _np
    import concourse.bacc as _bacc
    from concourse import mybir as _mybir
    from concourse.bass_utils import run_bass_kernel_spmd as _run

    v = {k: _np.asarray(a) for k, a in inputs.items()}
    L = "L0_gnn_"
    sent = {
        "adj": v["adj"].reshape(P, S, P, S)[:, ::-1, :, ::-1].transpose(2, 3, 1, 0).reshape(P, S * N),
        "adj_diag": v["adj"].diagonal().reshape(P, S)[:, ::-1],
        "x": v["x"].reshape(P, S, F)[:, ::-1],
        "WT": v[L + "W_gat"].T,
        "a2": v[L + "a_gat"].reshape(2, F).T,
        "wie": v[L + "w_ih_e"].T[0:F],
        "wie_neg": v[L + "w_ih_e"].T[F:2 * F],
        "whe": v[L + "w_hh_e"].T,
        "win": v[L + "w_ih_n"].T,
        "whn": v[L + "w_hh_n"].T,
        "bie": v[L + "b_ih_e"],
        "bhe": v[L + "b_hh_e"],
        "bin": v[L + "b_ih_n"],
        "bhn": v[L + "b_hh_n"],
        "w1": v["L1_gnn_weight"],
        "b1": v["L1_gnn_bias"],
    }
    nc = _bacc.Bacc("TRN2", target_bir_lowering=False, num_devices=1)
    arrays, args = {}, []
    for name in _ORDER:
        a = _np.ascontiguousarray(sent[name])
        arrays[f"in_{name}"] = a
        args.append(nc.dram_tensor(f"in_{name}", a.shape, _mybir.dt.from_np(a.dtype), kind="ExternalInput").ap())
    args.append(nc.dram_tensor("out_0", (P, S, F), F32, kind="ExternalOutput").ap())
    graph_layers(nc, *args)
    r = _run(nc, [arrays], core_ids=[0])
    return r.results[0]["out_0"][:, ::-1].reshape(N, F)
```

```python
from contextlib import ExitStack

import concourse.bass as bass
from concourse import mybir

F32 = mybir.dt.float32
BF16 = mybir.dt.bfloat16
I8 = mybir.dt.int8
U8 = mybir.dt.uint8
I16 = mybir.dt.int16
U16 = mybir.dt.uint16
I32 = mybir.dt.int32
ALU = mybir.AluOpType
ACT = mybir.ActivationFunctionType
AX_X = mybir.AxisListType.X

P = 128
N = 4096
F = 64
S = N // P
Q = 4
TW = N // Q
BANK = 512
NCH = N // BANK
BC = BANK // P
RING = 2 * Q
MASKS = 4
PARTS = 3
G = 3 * F
RZ = 2 * F
NODE, HID = G, 2 * G
WA = 2 * G + 2 * F
GROUPS = S // 2
ALPHA = 0.2
NEG_INF = -9.0e15
MAX_NEIGH = 100
UNIT = 128
FLAG = 128
HALF = N // 2
LEAD = 4
SCALE = 2.0 ** (127 - MAX_NEIGH)
EPS = 1e-5
LN_CHUNK = 8
DIAG_IT = 8
EARLY_IT, LATE_IT = 8, 12

GV, GA, GP = 13, 2, 9
ATT_EXP = 22


def graph_layers(nc, adj, adj_diag, x, WT, a2, wie, wie_neg, whe, win, whn, bie, bhe, bin_, bhn, w1, b1, out):
    assert MAX_NEIGH + 1 < FLAG - 1
    with ExitStack() as ctx:
        def sb(name, shape, dt):
            return ctx.enter_context(nc.sbuf_tensor(name, shape, dt))

        def sem(name):
            return ctx.enter_context(nc.semaphore(name))

        ps = ctx.enter_context(nc.psum_tensor("ps", [P, 8, BANK], F32))
        signs = sb("signs", [P, S * N], I8)
        tiles = sb("tiles", [P, RING * TW], F32)
        counts = sb("counts", [P, N], BF16)
        xs = sb("xs", [P, S, F], F32)
        h = sb("h", [P, S, F], F32)
        masks = sb("masks", [P, MASKS * TW], BF16)
        stage_f = sb("stage_f", [P, 2, F], F32)
        stage_b = sb("stage_b", [P, 4, G], BF16)
        ident = sb("ident", [P, P], F32)
        later = sb("later", [P, P], BF16)
        ones = sb("ones", [P, P], BF16)
        gru_w = sb("gru_w", [P, WA], F32)
        gate_w = sb("gate_w", [P, G], F32)
        score_w = sb("score_w", [P, 2], F32)
        w1_s = sb("w1_s", [F, F], F32)
        bias_rows = sb("bias_rows", [PARTS, WA], BF16)
        bias_1 = sb("bias_1", [P, F], F32)
        diag = sb("diag", [P, S], F32)
        sign_sum = sb("sign_sum", [P, S * Q], F32)
        stat = sb("stat", [P, 18, S], F32)
        full_room = sb("full_room", [P, 1], F32)
        done_mark = sb("done_mark", [1, 1], F32)
        flag_off = sb("flag_off", [P, 1], F32)
        ones_f = sb("ones_f", [P, 1], F32)
        excess = sb("excess", [P, 3], F32)
        flag = sb("flag", [1, 2], I32)
        longest = sb("longest", [P, 2], F32)
        rest = sb("rest", [P, RZ], F32)
        consts_t = sb("consts_t", [P, 4, LN_CHUNK], F32)
        rz_t = sb("rz_t", [P, 4 * RZ], F32)
        nn_t = sb("nn_t", [P, 4 * F], F32)
        dd_t = sb("dd_t", [P, 4 * F], F32)
        moments = sb("moments", [P, 2, 6], F32)
        mean_var = sb("mean_var", [P, 2, 2], F32)
        rs_nm = sb("rs_nm", [P, 2, 2], F32)
        kept_sums = nc.dram_tensor("kept_sums", (F, N), F32).ap()
        kept_room = nc.dram_tensor("kept_room", (P, N), U8).ap()

        def slots(ap):
            return ap.rearrange("p (s f) -> p s f", s=S)

        def early(slot, n):
            return signs[:, slot * N:slot * N + n * 4].bitcast(F32)

        mask_diag_h = slots(early(S - 5, S * F))
        adj_diag_h = slots(early(S - 7, S * F))
        cen = slots(early(S - 9, S * F))
        sq = slots(early(S - 11, S * F))
        bias_in = early(S - 12, 4 * G)[0:1, :]
        bias_all = early(S - 13, WA)[0:1, :]
        bias_parts = signs[0:1, (S - 14) * N:(S - 14) * N + 2 * PARTS * WA].bitcast(BF16)
        wt_s = early(S - 15, F)[0:F, :]
        a2_s = signs[0:F, (S - 15) * N + 512:(S - 15) * N + 520].bitcast(F32)
        win_s = signs[0:F, (S - 15) * N + 1024:(S - 15) * N + 1024 + 4 * G].bitcast(F32)
        X1 = tiles[:, 0:N]
        Y = tiles[0:F, N:2 * N]
        Yn = tiles[F:P, N:2 * N]
        AN = counts[:, :].bitcast(F32)
        WH = tiles[0:F, 0:N]
        room = masks[:, 0:N // 2].bitcast(U8)
        room_pairs = masks[:, 0:N // 2].bitcast(U16)
        codes = signs[:, :].bitcast(U8)
        pairs = signs[:, :].bitcast(U16)
        rz = rz_t[:, :].rearrange("p (b c f) -> p b c f", b=2, c=2)
        nn = nn_t[:, :].rearrange("p (b c f) -> p b c f", b=2, c=2)
        dd = dd_t[:, :].rearrange("p (b c f) -> p b c f", b=2, c=2)
        ss = rz_t[:, 0:RZ].rearrange("p (b f) -> p b f", b=2)
        added, x1_t = (nn_t[:, n * RZ:(n + 1) * RZ].rearrange("p (b f) -> p b f", b=2) for n in range(2))
        h2 = masks[:, N // 2:N // 2 + 2 * RZ].bitcast(F32)
        c_eps, c_half, c_scale, c_neg = (consts_t[:, n, :] for n in range(4))
        (mean, var, nz_d, neg_d, npos, has, ep, mx, en, e0, zz, pp, deg, nneg, n_zero, pm) = (
            stat[:, n, :] for n in range(16))
        term, rstd = mean, var
        neg_score = stat[:, 16:18, :].rearrange("p e s -> p (e s)").rearrange("p (s e) -> p s e", e=2)

        names = """diag_loaded w_loaded gru_w_loaded bias_loaded bias_moved consts bias_step
            prep rstd_step h_ready diag_done small_w small_w_out counts_step masks_made signs_kept
            masks_used tiles_used sums_done staged moved moved_a turned turned_out scores att att_exp
            att_final spread mixed behind room_ready gru_pe gru_v gru_a gru_p marked coded room_step
            weighed weights_used bias_added wh_out projected final stored degrees flag_step excess_sum
            flag_ready neg_saved neg_loaded neg_v neg_used neg_reloaded neg_out neg_scores neg_spread
            neg_mixed neg_gates long_step
            normed_x1""".split()
        (diag_loaded, w_loaded, gru_w_loaded, bias_loaded, bias_moved, consts, bias_step,
         prep, rstd_step, h_ready, diag_done, small_w, small_w_out, counts_step, masks_made, signs_kept,
         masks_used, tiles_used, sums_done, staged, moved, moved_a, turned, turned_out, scores, att, att_exp,
         att_final, spread, mixed, behind, room_ready, gru_pe, gru_v, gru_a, gru_p, marked, coded, room_step,
         weighed, weights_used, bias_added, wh_out, projected, final, stored, degrees, flag_step, excess_sum,
         flag_ready, neg_saved, neg_loaded, neg_v, neg_used, neg_reloaded, neg_out, neg_scores, neg_spread,
         neg_mixed, neg_gates, long_step,
         normed_x1) = map(sem, names)
        x_loaded = [sem(f"x_loaded{c}") for c in range(S // LN_CHUNK)]
        tile_loaded = [sem(f"tile_loaded{u}") for u in range(RING)]
        N_CONST = 16

        def load_flag(eng, name, n):
            reg = eng.alloc_register(name)
            eng.wait_ge(flag_ready, 1)
            eng.reg_load(reg, flag[0:1, n:n + 1])
            return reg

        def weights(g, odd, half):
            aside = odd and not (isinstance(g, int) and g == 0)
            ring = (signs[:, 0:2 * N] if aside else counts[:, :]).bitcast(I16)
            return ring[:, half * HALF:(half + 1) * HALF]

        def sums_of(c):
            return c // 2, slice(F * (c % 2), F * (c % 2) + F)

        def chunk(c):
            return slice(c * BANK, (c + 1) * BANK)

        block = ctx.enter_context(nc.Block())

        @block.sync
        def _(sp):
            for c in range(S // LN_CHUNK):
                part = slice(c * LN_CHUNK, (c + 1) * LN_CHUNK)
                sp.dma_start(xs[:, part, :], x[:, part, :]).then_inc(x_loaded[c], 16)
                for u in range(2 * c, 2 * c + 2):
                    sp.dma_start(tiles[:, u * TW:(u + 1) * TW], adj[:, u * TW:(u + 1) * TW])\
                        .then_inc(tile_loaded[u], 16)
            with sp.Fori(1, S // 2) as it:
                for u in range(RING):
                    sp.wait_ge(tiles_used, it * RING + (u + 1 - RING))
                    sp.wait_ge(masks_made, it * RING + (u + 1 - RING))
                    sp.wait_ge(signs_kept, it * RING + (u + 1 - RING))
                    sp.dma_start(tiles[:, u * TW:(u + 1) * TW],
                                 adj[:, bass.ds(it * (2 * N) + u * TW, TW)]).then_inc(tile_loaded[u], 16)

            has_neg = load_flag(sp, "sp_neg", 0)
            with sp.If_ne(has_neg, 0):
                sp.wait_ge(moved, NCH)
                sp.wait_ge(room_ready, NCH)
                sp.dma_start(kept_sums, X1[0:F, :]).then_inc(neg_saved, 16)
                sp.dma_start(kept_room, room).then_inc(neg_saved, 16)
                sp.wait_ge(neg_saved, 32)
                with sp.Fori(0, S) as s:
                    sp.wait_ge(neg_used, s + 1)
                    sp.dma_start(tiles[:, 0:N], adj[:, bass.ds(s * N, N)]).then_inc(neg_loaded, 16)
                sp.wait_ge(neg_used, S + 1)
                sp.dma_start(X1[0:F, :], kept_sums).then_inc(neg_reloaded, 16)
                sp.dma_start(room, kept_room).then_inc(neg_reloaded, 16)

            for q in range(Q):
                part = slice(q * (S // Q), (q + 1) * (S // Q))
                sp.wait_ge(final, q + 1)
                sp.dma_start(out[:, part, :], xs[:, part, :]).then_inc(stored, 16)
            sp.wait_ge(stored, 16 * Q)

        @block.gpsimd
        def _(pool):
            for ap, value in ((c_eps, EPS), (c_half, -0.5), (c_scale, SCALE), (c_neg, -1.0), (ident[:, :], 1.0),
                              (later[:, :], -1.0), (ones[:, :], 1.0),
                              (full_room[:, :], float(MAX_NEIGH + 1)),
                              (flag_off[:, :], -float(UNIT * FLAG)), (gru_w[:, :], 0.0),
                              (ones_f[:, :], 1.0), (nneg, 0.0), (stat[:, 16:18, :], 0.0), (flag[:, :], 0)):
                pool.memset(ap, value).then_inc(consts, 1)
            pool.wait_ge(consts, N_CONST - 2)
            pool.affine_select(out=ident[:, :], in_=ident[:, :], compare_op=ALU.is_equal, fill=0.0, base=0,
                               pattern=[[-1, P]], channel_multiplier=1).then_inc(consts, 1)
            pool.affine_select(out=later[:, :], in_=later[:, :], compare_op=ALU.is_gt, fill=0.0, base=0,
                               pattern=[[-1, P]], channel_multiplier=1).then_inc(consts, 1)

            def deviation(c):
                v = var[:, c * LN_CHUNK:(c + 1) * LN_CHUNK]
                pool.wait_ge(prep, 1 + 6 * (c + 1))
                pool.tensor_tensor(v, v, c_eps, ALU.add).then_inc(rstd_step, 1)
                pool.wait_ge(rstd_step, 2 * c + 1)
                pool.tensor_tensor(v, v, c_half, ALU.pow).then_inc(rstd_step, 1)

            def stage(it):
                for k in range(2):
                    if not (isinstance(it, int) and it == 0):
                        pool.wait_ge(tiles_used, it * RING + ((k + 1) * Q - RING))
                    hs = stage_f[:, k, :]
                    hi, mid, lo = (stage_b[:, k, n * F:(n + 1) * F] for n in range(PARTS))
                    base = it * 10 + 5 * k
                    pool.tensor_copy(hs, h[:, bass.ds(it * 2 + k, 1), :].rearrange("p a f -> p (a f)"))\
                        .then_inc(staged, 1)
                    pool.wait_ge(staged, base + 1)
                    pool.tensor_tensor(hi, hs, ones[:, 0:F], ALU.mult).then_inc(staged, 1)
                    pool.wait_ge(staged, base + 2)
                    pool.tensor_tensor(rest[:, 0:F], hs, hi, ALU.subtract).then_inc(staged, 1)
                    pool.wait_ge(staged, base + 3)
                    pool.tensor_tensor(mid, rest[:, 0:F], ones[:, 0:F], ALU.mult).then_inc(staged, 1)
                    pool.wait_ge(staged, base + 4)
                    pool.tensor_tensor(lo, rest[:, 0:F], mid, ALU.subtract).then_inc(staged, 1)

            deviation(0)
            pool.wait_ge(h_ready, 1)
            stage(0)
            pool.wait_ge(bias_loaded, 16 * 4)
            be_i, be_h, bn_i, bn_h = (bias_in[:, n * G:(n + 1) * G] for n in range(4))
            for at, bi, bh in ((0, be_i, be_h), (NODE, bn_i, bn_h)):
                pool.tensor_copy(bias_all[:, at:at + F], bi[:, RZ:G]).then_inc(bias_step, 1)
                pool.tensor_tensor(bias_all[:, at + F:at + G], bi[:, 0:RZ], bh[:, 0:RZ], ALU.add).then_inc(bias_step, 1)
            pool.tensor_copy(bias_all[:, HID:HID + F], be_h[:, RZ:G]).then_inc(bias_step, 1)
            pool.tensor_copy(bias_all[:, HID + F:WA], bn_h[:, RZ:G]).then_inc(bias_step, 1)
            pool.wait_ge(bias_step, 6)
            for part in range(PARTS):
                piece = bias_parts[:, part * WA:(part + 1) * WA]
                pool.tensor_copy(piece, bias_all[:, :]).then_inc(bias_step, 1)
                pool.wait_ge(bias_step, 7 + 2 * part)
                if part < PARTS - 1:
                    pool.tensor_tensor(bias_all[:, :], bias_all[:, :], piece, ALU.subtract).then_inc(bias_step, 1)
                    pool.wait_ge(bias_step, 8 + 2 * part)
            for c in range(1, S // LN_CHUNK):
                deviation(c)
                stage(c)
            pool.wait_ge(h_ready, S // LN_CHUNK)
            with pool.Fori(S // LN_CHUNK, S // 2) as it:
                stage(it)

            def norm(g, par):
                two = slice(0, 2)
                rs, nm = rs_nm[:, 0, :], rs_nm[:, 1, :]
                hi, mid, lo = (stage_b[:, 2 * par:2 * par + 2, n * F:(n + 1) * F] for n in range(PARTS))
                h2v, rv = (t.rearrange("p (b f) -> p b f", b=2) for t in (h2, rest[:, :]))
                one = ones[:, :].rearrange("p (b f) -> p b f", b=2)

                def after(k):
                    pool.wait_ge(gru_p, g * GP + k)

                pool.wait_ge(gru_v, g * GV + GV)
                pool.tensor_tensor(rs, mean_var[:, :, 1], c_eps[:, two], ALU.add).then_inc(gru_p, 1)
                after(1)
                pool.tensor_tensor(rs, rs, c_half[:, two], ALU.pow).then_inc(gru_p, 1)
                after(2)
                pool.tensor_tensor(rs, rs, c_scale[:, two], ALU.mult).then_inc(gru_p, 1)
                after(3)
                pool.tensor_tensor(nm, mean_var[:, :, 0], rs, ALU.mult).then_inc(gru_p, 1)
                after(4)
                pool.tensor_tensor(nm, nm, c_neg[:, two], ALU.mult).then_inc(gru_p, 1)
                pool.wait_ge(normed_x1, g * 2 + 2)
                if not (isinstance(g, int) and g < 2):
                    pool.wait_ge(weights_used, g * 4 - 4)
                pool.tensor_tensor(hi, h2v, one, ALU.mult).then_inc(gru_p, 1)
                after(6)
                pool.tensor_tensor(rv, h2v, hi, ALU.subtract).then_inc(gru_p, 1)
                after(7)
                pool.tensor_tensor(mid, rv, one, ALU.mult).then_inc(gru_p, 1)
                after(8)
                pool.tensor_tensor(lo, rv, mid, ALU.subtract).then_inc(gru_p, 1)

            pool.wait_ge(att_final, 1)
            norm(0, 0)
            norm(1, 1)
            with pool.Fori(1, GROUPS // 2) as it:
                norm(it * 2, 0)
                norm(it * 2 + 1, 1)
            pool.tensor_tensor(xs[:, :, :], xs[:, :, :], bias_1[:, None, :].to_broadcast((P, S, F)), ALU.add)\
                .then_inc(bias_added, 1)

        @block.scalar
        def _(act):
            for dst, src in ((wt_s, WT), (a2_s, a2), (win_s[:, 0:F], win[:, RZ:G]), (win_s[:, F:G], win[:, 0:RZ])):
                act.dma_start(dst, src).then_inc(w_loaded, 16)
            act.dma_start(diag[:, :], adj_diag).then_inc(diag_loaded, 16)
            for n, b in enumerate((bie, bhe, bin_, bhn)):
                act.dma_start(bias_in[:, n * G:(n + 1) * G], b.rearrange("(a n) -> a n", a=1)).then_inc(bias_loaded, 16)
            act.wait_ge(consts, N_CONST)
            for dst, src in ((gru_w[0:F, 0:F], wie[:, RZ:G]), (gru_w[0:F, F:G], wie[:, 0:RZ]),
                             (gru_w[F:P, F:G], whe[:, 0:RZ]), (gru_w[F:P, HID:HID + F], whe[:, RZ:G]),
                             (gru_w[F:P, NODE + F:HID], whn[:, 0:RZ]), (gru_w[F:P, HID + F:WA], whn[:, RZ:G]),
                             (gate_w[F:P, 0:F], wie_neg[:, RZ:G]), (gate_w[F:P, F:G], wie_neg[:, 0:RZ]),
                             (w1_s[:, :], w1), (bias_1[:, :], bass.AP(tensor=b1.tensor, offset=0, ap=[[0, P], [1, F]]))):
                act.dma_start(dst, src).then_inc(gru_w_loaded, 16)

            def keep_signs(it):
                for u in range(RING):
                    act.wait_ge(tile_loaded[u], it * 16 + 16)
                    act.activation(signs[:, bass.ds(it * (2 * N) + u * TW, TW)], tiles[:, u * TW:(u + 1) * TW],
                                   ACT.Sign, accum_out=sign_sum[:, bass.ds(it * RING + u, 1)]).then_inc(signs_kept, 1)

            keep_signs(0)
            act.wait_ge(bias_step, 11)
            act.dma_start(bias_rows[:, :], bias_parts.rearrange("a (r n) -> a r n", r=PARTS)).then_inc(bias_moved, 16)
            with act.Fori(1, EARLY_IT) as it:
                keep_signs(it)
            act.wait_ge(h_ready, S // LN_CHUNK)
            act.wait_ge(small_w_out, 3)
            act.wait_ge(bias_moved, 16)
            with act.Fori(EARLY_IT, LATE_IT) as it:
                keep_signs(it)
            act.wait_ge(sums_done, 1)
            with act.Fori(LATE_IT, S // 2) as it:
                keep_signs(it)

            act.wait_ge(tiles_used, S * Q)
            act.wait_ge(masks_made, S * Q)
            act.wait_ge(signs_kept, S * Q)
            for c in (2, 3, 0, 1, 6, 7, 4, 5):
                b, rows = sums_of(c)
                act.activation(Y[:, chunk(c)], ps[rows, Q + b, :], ACT.Copy).then_inc(moved_a, 1)
            for c in range(NCH):
                act.wait_ge(behind, c + 1)
                act.activation(room[:, chunk(c)], ps[:, 6 + c % 2, :], ACT.Relu, bias=full_room[:, :])                    .then_inc(room_ready, 1)

            def turn_out(c):
                b, rows = sums_of(c)
                act.wait_ge(turned, c + 1)
                act.activation(X1[F:P, chunk(c)], ps[rows, b, :], ACT.Copy).then_inc(turned_out, 1)

            for c in range(4):
                turn_out(c)
            for e in (ep, en, e0):
                act.wait_ge(att, ATT_EXP)
                act.activation(e, e, ACT.Exp).then_inc(att_exp, 1)
            for c in range(4, NCH):
                turn_out(c)

            def weigh(g, odd, half):
                place = weights(g, odd, half)
                n = g * 4 + (odd * 2 + half)
                act.wait_ge(coded, n + 1)
                if not isinstance(g, int) or g > 1:
                    act.wait_ge(weights_used, n - 3)
                elif g == 1 and odd:
                    act.wait_ge(weighed, 4)
                elif (g, odd) != (0, 0):
                    act.wait_ge(weights_used, n - 1)
                act.activation(place, codes[:, bass.ds(g * (2 * N) + (odd * N + half * HALF), HALF)], ACT.Relu,
                               bias=flag_off[:, :], scale=float(UNIT)).then_inc(weighed, 1)

            def gates(g, par):
                A = ps[:, 6 - 2 * par:8 - 2 * par, 0:HID].rearrange("p b (c f) -> p b c f", c=2)
                act.wait_ge(gru_pe, g + 1)
                if not (isinstance(g, int) and g == 0):
                    act.wait_ge(gru_v, g * GV - 2)
                act.activation(rz[:, :, :, :], A[:, :, :, F:G], ACT.Sigmoid).then_inc(gru_a, 1)

            def candidates(g):
                act.wait_ge(gru_v, g * GV + 2)
                act.activation(nn[:, :, :, :], nn[:, :, :, :], ACT.Tanh).then_inc(gru_a, 1)

            def normed(g, par):
                act.wait_ge(gru_p, g * GP + 5)
                for b in range(2):
                    act.activation(h2[:, b * F:(b + 1) * F],
                                   xs[:, bass.ds(g * 2 + b, 1), :].rearrange("p a f -> p (a f)"), ACT.Relu,
                                   bias=rs_nm[:, 1, b:b + 1], scale=rs_nm[:, 0, b:b + 1]).then_inc(normed_x1, 1)

            def group(g, par):
                static = isinstance(g, int)
                if not static or g < GROUPS:
                    gates(g, par)
                if not static or g >= 2:
                    weigh(g - 2, 0, 1)
                if not static or g < GROUPS:
                    candidates(g)
                if not static or g >= 2:
                    weigh(g - 2, 1, 0)
                if not static or 1 <= g <= GROUPS:
                    normed(g - 1, 1 - par)
                if not static or g >= 2:
                    weigh(g - 2, 1, 1)
                if not static or 1 <= g <= GROUPS:
                    weigh(g - 1, 0, 0)

            act.wait_ge(att_final, 1)
            act.wait_ge(behind, NCH)
            has_neg = load_flag(act, "act_neg", 0)
            with act.If_ne(has_neg, 0):
                act.wait_ge(neg_mixed, 2 * NCH)
            for g in range(4):
                group(g, g % 2)
            with act.Fori(2, GROUPS // 2) as it:
                group(it * 2, 0)
                group(it * 2 + 1, 1)
            group(GROUPS, 0)
            group(GROUPS + 1, 1)
            for c in range(0, NCH, 2):
                act.wait_ge(weights_used, 2 * S - 1 + c // 4)
                act.activation(WH[:, chunk(c)], ps[0:F, c // 2, :], ACT.Copy).then_inc(wh_out, 1)

        @block.vector
        def _(dve):
            seen = {}

            def link(ins, s):
                seen[s.name] = seen.get(s.name, 0) + 1
                ins.then_inc(s, 1)
                dve.wait_ge(s, seen[s.name])
                return seen[s.name]

            def wide(v, n):
                return v[:, :, None].to_broadcast((P, n, F))

            link(dve.memset(counts[:, :].bitcast(F32), 0.0), prep)

            def normalise(c):
                part = slice(c * LN_CHUNK, (c + 1) * LN_CHUNK)
                xc, cc, m, v = xs[:, part, :], cen[:, part, :], mean[:, part], var[:, part]
                dve.wait_ge(x_loaded[c], 16)
                link(dve.tensor_reduce(m, xc, AX_X, ALU.add), prep)
                link(dve.tensor_scalar(m, m, 1.0 / F, None, ALU.mult), prep)
                link(dve.tensor_tensor(cc, xc, wide(m, LN_CHUNK), ALU.subtract), prep)
                link(dve.tensor_tensor(sq[:, part, :], cc, cc, ALU.mult), prep)
                link(dve.tensor_reduce(v, sq[:, part, :], AX_X, ALU.add), prep)
                link(dve.tensor_scalar(v, v, 1.0 / F, None, ALU.mult), prep)
                dve.wait_ge(rstd_step, 2 * (c + 1))
                dve.scalar_tensor_tensor(out=h[:, part, :], in0=cc, scalar=0.0, in1=wide(v, LN_CHUNK),
                                         op0=ALU.max, op1=ALU.mult).then_inc(h_ready, 1)

            def make_masks(it):
                first = isinstance(it, int) and it == 0
                for u in range(0, RING, 2):
                    for v in (u, u + 1):
                        dve.wait_ge(tile_loaded[v], it * 16 + 16)
                        if not (first and v < MASKS):
                            dve.wait_ge(masks_used, it * RING + (v + 1 - MASKS))
                            dve.wait_ge(counts_step, it * RING + (v + 1 - MASKS))
                        dve.tensor_scalar(masks[:, (v % MASKS) * TW:(v % MASKS + 1) * TW],
                                          tiles[:, v * TW:(v + 1) * TW], 0.0, None, ALU.not_equal)\
                            .then_inc(masks_made, 1)
                    for v in (u, u + 1):
                        dve.wait_ge(masks_made, it * RING + (v + 1))
                        if not (first and v < Q):
                            dve.wait_ge(counts_step, it * RING + (v + 1 - Q))
                        part = counts[:, (v % Q) * TW:(v % Q + 1) * TW]
                        dve.tensor_tensor(part, part, masks[:, (v % MASKS) * TW:(v % MASKS + 1) * TW], ALU.add)\
                            .then_inc(counts_step, 1)
                    dve.wait_ge(signs_kept, it * RING + (u + 2))
                    kept = pairs[:, bass.ds(it * N + u * (TW // 2), TW)]
                    dve.tensor_scalar(kept, kept, float(FLAG - 1), None, ALU.mult).then_inc(marked, 1)

            normalise(0)
            make_masks(0)
            dve.wait_ge(small_w, 1)
            dve.tensor_copy(gate_w[0:F, :], ps[0:F, 7, 0:G]).then_inc(small_w_out, 1)
            for k in (0, F):
                dve.tensor_copy(score_w[k:k + F, :], ps[0:F, 7, G:G + 2]).then_inc(small_w_out, 1)
            for c in range(1, S // LN_CHUNK):
                normalise(c)
                make_masks(c)
            dve.wait_ge(diag_loaded, 16)
            dve.wait_ge(h_ready, S // LN_CHUNK)
            link(dve.tensor_scalar(nz_d, diag[:, :], 0.0, -1.0, ALU.not_equal, ALU.mult), prep)
            link(dve.tensor_scalar(neg_d, diag[:, :], -1.0, None, ALU.mult), prep)
            dve.tensor_tensor(mask_diag_h, h[:, :, :], wide(nz_d, S), ALU.mult).then_inc(diag_done, 1)
            make_masks(S // LN_CHUNK)
            dve.tensor_tensor(adj_diag_h, h[:, :, :], wide(neg_d, S), ALU.mult).then_inc(diag_done, 1)
            with dve.Fori(S // LN_CHUNK + 1, S // 2) as it:
                make_masks(it)

            dve.wait_ge(tiles_used, S * Q)
            dve.wait_ge(masks_made, S * Q)
            dve.wait_ge(signs_kept, S * Q)
            def move(c):
                b, rows = sums_of(c)
                dve.tensor_copy(X1[0:F, chunk(c)], ps[rows, b, :]).then_inc(moved, 1)

            for c in range(3):
                move(c)

            dve.wait_ge(degrees, 1)
            dve.wait_ge(consts, N_CONST)
            link(dve.tensor_copy(deg, ps[:, 5, 2 * S:3 * S]), flag_step)
            link(dve.tensor_reduce(excess[:, 0:1], deg, AX_X, ALU.add), flag_step)
            link(dve.tensor_reduce(excess[:, 1:2], sign_sum[:, :], AX_X, ALU.add), flag_step)
            link(dve.tensor_tensor(excess[:, 2:3], excess[:, 0:1], excess[:, 1:2], ALU.subtract), flag_step)
            link(dve.tensor_scalar(has, deg, float(MAX_NEIGH), None, ALU.is_gt), flag_step)
            link(dve.tensor_reduce(longest[:, 0:1], has, AX_X, ALU.add), flag_step)
            for c in range(3, NCH):
                move(c)
            dve.wait_ge(excess_sum, 2)
            dve.tensor_copy(flag[:, :], ps[0:1, 5, 0:2]).then_inc(flag_ready, 1)

            has_neg = load_flag(dve, "dve_neg", 0)
            has_long = load_flag(dve, "dve_long", 1)
            with dve.If_ne(has_neg, 0):
                dve.wait_ge(neg_saved, 32)
                dve.memset(counts[:, :], 0.0).then_inc(neg_v, 1)
                dve.wait_ge(neg_v, 1)
                with dve.Fori(0, S) as s:
                    dve.wait_ge(neg_loaded, s * 16 + 16)
                    dve.wait_ge(neg_used, s + 1)
                    hs = h[:, bass.ds(s, 1), :].rearrange("p a f -> p (a f)")
                    own = tiles[:, bass.ds(s * P, P)]
                    dve.tensor_scalar(signs[:, bass.ds(s * N, N)], tiles[:, 0:N], 0.0, float(FLAG - 1),
                                      ALU.not_equal, ALU.mult).then_inc(neg_v, 1)
                    dve.wait_ge(neg_v, s * 10 + 2)
                    dve.tensor_scalar(stage_f[:, 0, :], hs, 1.0, None, ALU.mult).then_inc(neg_v, 1)
                    dve.tensor_scalar(stage_b[:, 0, 0:F], hs, 1.0, None, ALU.mult).then_inc(neg_v, 1)
                    dve.scalar_tensor_tensor(out=own, in0=ident[:, :], scalar=0.0, in1=own, op0=ALU.is_equal,
                                             op1=ALU.mult).then_inc(neg_v, 1)
                    dve.wait_ge(neg_v, s * 10 + 5)
                    dve.tensor_tensor(stage_f[:, 1, :], stage_f[:, 0, :], stage_b[:, 0, 0:F], ALU.subtract)                        .then_inc(neg_v, 1)
                    dve.wait_ge(neg_v, s * 10 + 6)
                    dve.tensor_scalar(stage_b[:, 0, F:2 * F], stage_f[:, 1, :], 1.0, None, ALU.mult).then_inc(neg_v, 1)
                    dve.wait_ge(neg_v, s * 10 + 7)
                    dve.tensor_tensor(stage_b[:, 0, 2 * F:G], stage_f[:, 1, :], stage_b[:, 0, F:2 * F], ALU.subtract)                        .then_inc(neg_v, 1)
                    dve.tensor_scalar(masks[:, :], tiles[:, 0:N], 0.0, None, ALU.is_lt).then_inc(neg_v, 1)
                    dve.wait_ge(neg_v, s * 10 + 9)
                    dve.tensor_scalar(tiles[:, 0:N], tiles[:, 0:N], 0.0, None, ALU.min).then_inc(neg_v, 1)
                    dve.tensor_tensor(counts[:, :], counts[:, :], masks[:, :], ALU.add).then_inc(neg_v, 1)
                    dve.wait_ge(neg_v, s * 10 + 11)
                dve.wait_ge(neg_used, S + 1)
                dve.wait_ge(neg_reloaded, 32)
                dve.wait_ge(moved_a, NCH)
                for c in range(NCH):
                    b, rows = sums_of(c)
                    at = chunk(c)
                    dve.tensor_copy(Yn[:, at], ps[rows, b, :]).then_inc(neg_out, 1)
                    dve.tensor_tensor(X1[0:F, at], X1[0:F, at], ps[rows, b, :], ALU.subtract).then_inc(neg_out, 1)
                    dve.tensor_tensor(Y[:, at], Y[:, at], ps[rows, Q + b, :], ALU.subtract).then_inc(neg_out, 1)
                dve.wait_ge(neg_out, 3 * NCH)
                dve.wait_ge(neg_scores, 1)
                dve.tensor_copy(neg_score, ps[:, 0, 0:2 * S].rearrange("p (s e) -> p s e", e=2)).then_inc(neg_out, 1)
                dve.tensor_copy(nneg, ps[:, 0, 2 * S:3 * S]).then_inc(neg_out, 1)
                dve.tensor_copy(AN, ps[:, Q:2 * Q, :].rearrange("p b n -> p (b n)")).then_inc(neg_out, 1)
                dve.wait_ge(neg_out, 3 * NCH + 3)
                dve.wait_ge(neg_scores, 2)

            def code(slot):
                for v in range(2):
                    if not (isinstance(slot, int) and slot == 0):
                        dve.wait_ge(room_step, slot * 2 + (v - 1))
                    half = pairs[:, bass.ds(slot * (N // 2) + v * (HALF // 2), HALF // 2)]
                    dve.tensor_tensor(half, room_pairs[:, v * (HALF // 2):(v + 1) * (HALF // 2)], half, ALU.add)                        .then_inc(coded, 1)
                for v in range(2):
                    dve.wait_ge(coded, slot * 2 + (v + 1))
                    half = pairs[:, bass.ds(slot * (N // 2) + v * (HALF // 2), HALF // 2)]
                    dve.tensor_scalar(room_pairs[:, v * (HALF // 2):(v + 1) * (HALF // 2)], half,
                                      (FLAG - 1) * 257, None, ALU.bitwise_and).then_inc(room_step, 1)
                with dve.If_ne(has_long, 0):
                    dve.wait_ge(room_step, slot * 2 + 2)
                    dve.scalar_tensor_tensor(out=room, in0=room, scalar=float(FLAG - 1), in1=room,
                                             op0=ALU.not_equal, op1=ALU.mult).then_inc(long_step, 1)
                    dve.wait_ge(long_step, slot + 1)
                    dve.memset(done_mark[:, :], 0.0)

            dve.wait_ge(room_ready, NCH)
            for slot in range(2):
                code(slot)

            dve.wait_ge(scores, 1)
            E = ps[:, 4, 0:2 * S].rearrange("p (s e) -> p s e", e=2)
            link(dve.tensor_tensor(npos, deg, nz_d, ALU.add), att)
            link(dve.tensor_scalar(n_zero, npos, -1.0, float(N), ALU.mult, ALU.add), att)
            link(dve.tensor_tensor(npos, npos, nneg, ALU.subtract), att)
            for e, own, other, many in ((ep, 0, 1, npos), (en, 1, 0, nneg)):
                link(dve.tensor_tensor(e, E[:, :, own], neg_score[:, :, other], ALU.add), att)
                link(dve.tensor_scalar(term, e, ALPHA, None, ALU.mult), att)
                link(dve.tensor_tensor(e, e, term, ALU.max), att)
                link(dve.tensor_scalar(has, many, 0.5, None, ALU.is_ge), att)
                link(dve.tensor_tensor(e, e, has, ALU.mult), att)
                link(dve.tensor_scalar(has, has, 1.0, -NEG_INF, ALU.subtract, ALU.mult), att)
                link(dve.tensor_tensor(e, e, has, ALU.add), att)
            link(dve.tensor_tensor(mx, ep, en, ALU.max), att)
            link(dve.tensor_scalar(mx, mx, NEG_INF, None, ALU.max), att)
            link(dve.tensor_tensor(ep, ep, mx, ALU.subtract), att)
            link(dve.tensor_tensor(en, en, mx, ALU.subtract), att)
            n = link(dve.tensor_scalar(e0, mx, -1.0, NEG_INF, ALU.mult, ALU.add), att)
            assert n == ATT_EXP

            code(2)
            dve.wait_ge(att_exp, 3)
            link(dve.tensor_tensor(zz, ep, npos, ALU.mult), att)
            link(dve.tensor_tensor(term, en, nneg, ALU.mult), att)
            link(dve.tensor_tensor(zz, zz, term, ALU.add), att)
            link(dve.tensor_tensor(e0, e0, n_zero, ALU.mult), att)
            link(dve.tensor_tensor(zz, zz, e0, ALU.add), att)
            link(dve.reciprocal(zz, zz), att)
            link(dve.tensor_tensor(pp, ep, zz, ALU.mult), att)
            dve.tensor_tensor(pm, en, zz, ALU.mult).then_inc(att_final, 1)
            for c in range(NCH):
                b, rows = sums_of(c)
                at = chunk(c)
                dve.wait_ge(spread, c + 1)
                dve.tensor_tensor(Y[:, at], Y[:, at], ps[rows, b, :], ALU.mult).then_inc(mixed, 1)
                with dve.If_ne(has_neg, 0):
                    dve.wait_ge(mixed, c + 1)
                    dve.wait_ge(neg_spread, c + 1)
                    dve.tensor_tensor(ps[rows, b, :], AN[rows, b * BANK:(b + 1) * BANK], ps[rows, b, :], ALU.mult)                        .then_inc(neg_mixed, 1)
                    dve.wait_ge(neg_mixed, 2 * c + 1)
                    dve.tensor_tensor(Y[:, at], Y[:, at], ps[rows, b, :], ALU.add).then_inc(neg_mixed, 1)
                    dve.wait_ge(neg_mixed, 2 * c + 2)
            code(3)

            def candidates(g, par):
                A = ps[:, 6 - 2 * par:8 - 2 * par, :]
                ins = A[:, :, 0:HID].rearrange("p b (c f) -> p b c f", c=2)[:, :, :, 0:F]
                hid = A[:, :, HID:WA].rearrange("p b (c f) -> p b c f", c=2)
                dve.wait_ge(gru_a, g * GA + 1)
                dve.tensor_tensor(nn[:, :, :, :], rz[:, :, :, 0:F], hid, ALU.mult).then_inc(gru_v, 1)
                dve.wait_ge(gru_v, g * GV + 1)
                dve.tensor_tensor(nn[:, :, :, :], nn[:, :, :, :], ins, ALU.add).then_inc(gru_v, 1)

            def states(g):
                hk = h[:, bass.ds(g * 2, 2), :][:, :, None, :].to_broadcast((P, 2, 2, F))
                dve.wait_ge(gru_a, g * GA + 2)
                dve.tensor_tensor(dd[:, :, :, :], hk, nn[:, :, :, :], ALU.subtract).then_inc(gru_v, 1)
                dve.wait_ge(gru_v, g * GV + 3)
                dve.tensor_tensor(dd[:, :, :, :], dd[:, :, :, :], rz[:, :, :, F:RZ], ALU.mult).then_inc(gru_v, 1)
                dve.wait_ge(gru_v, g * GV + 4)
                dve.tensor_tensor(dd[:, :, :, :], dd[:, :, :, :], nn[:, :, :, :], ALU.add).then_inc(gru_v, 1)
                dve.wait_ge(gru_v, g * GV + 5)
                dve.tensor_tensor(ss, dd[:, :, 0, :], dd[:, :, 1, :], ALU.add).then_inc(gru_v, 1)
                dve.wait_ge(gru_v, g * GV + 6)
                xk = xs[:, bass.ds(g * 2, 2), :]
                dk = diag[:, bass.ds(g * 2, 2)][:, :, None].to_broadcast((P, 2, F))
                dve.tensor_tensor(added, ss, dk, ALU.mult).then_inc(gru_v, 1)
                dve.wait_ge(gru_v, g * GV + 7)
                dve.tensor_tensor(x1_t, added, xk, ALU.add).then_inc(gru_v, 1)
                for b in range(2):
                    dve.wait_ge(gru_v, g * GV + 8)
                    dve.bn_stats(moments[:, b, :], x1_t[:, b, :]).then_inc(gru_v, 1)
                if not (isinstance(g, int) and g == 0):
                    dve.wait_ge(gru_p, g * GP - 5)
                dve.wait_ge(gru_v, g * GV + 10)
                dve.tensor_tensor(xk, added, xk, ALU.add).then_inc(gru_v, 1)
                for b in range(2):
                    dve.bn_aggr(mean_var[:, b, :], moments[:, b, :]).then_inc(gru_v, 1)

            def group(g, par, more):
                candidates(g, par)
                if more:
                    code(g * 2 + (LEAD - 2))
                states(g)
                if more:
                    code(g * 2 + (LEAD - 1))

            LAST = GROUPS - LEAD // 2 + 1
            group(0, 0, False)
            with dve.Fori(0, (LAST - 1) // 2) as it:
                group(it * 2 + 1, 1, True)
                group(it * 2 + 2, 0, True)
            for g in range(LAST, GROUPS):
                group(g, g % 2, False)

            for c in range(1, NCH, 2):
                dve.wait_ge(weights_used, 2 * S - 1 + c // 4)
                dve.tensor_copy(WH[:, chunk(c)], ps[F:P, c // 2, :]).then_inc(wh_out, 1)
            dve.wait_ge(bias_added, 1)
            for q in range(Q):
                dve.wait_ge(projected, q + 1)
                xq = xs[:, q * (S // Q):(q + 1) * (S // Q), :]
                dve.tensor_tensor(xq, ps[:, Q + q, :].rearrange("p (s f) -> p s f", f=F), xq, ALU.add)\
                    .then_inc(final, 1)

        @block.tensor
        def _(pe):
            def mm(dst, lhsT, rhs, start=False, stop=False):
                return pe.matmul(dst, lhsT, rhs, start=start, stop=stop, skip_group_check=True)

            pe.wait_ge(w_loaded, 16 * 4)
            mm(ps[0:F, 7, 0:G], wt_s, win_s, True, True)
            mm(ps[0:F, 7, G:G + 2], wt_s, a2_s, True, True).then_inc(small_w, 1)
            pe.wait_ge(consts, N_CONST)

            def products(it):
                begin = isinstance(it, int) and it == 0
                for u in range(RING):
                    k, q = divmod(u, Q)
                    if q == 0:
                        pe.wait_ge(staged, it * 10 + (5 * k + 5))
                    first = begin and k == 0
                    pe.wait_ge(masks_made, it * RING + (u + 1))
                    m = masks[:, (u % MASKS) * TW:(u % MASKS + 1) * TW]
                    for part in range(PARTS):
                        for c in range(2):
                            last = mm(ps[c * F:(c + 1) * F, q, :], stage_b[:, k, part * F:(part + 1) * F],
                                      m[:, c * BANK:(c + 1) * BANK], first and part == 0)
                    last.then_inc(masks_used, 1)
                    pe.wait_ge(tile_loaded[u], it * 16 + 16)
                    if first and Q + q == 7:
                        pe.wait_ge(small_w_out, 3)
                    for c in range(2):
                        last = mm(ps[c * F:(c + 1) * F, Q + q, :], stage_f[:, k, :],
                                  tiles[:, u * TW + c * BANK:u * TW + (c + 1) * BANK], first)
                    last.then_inc(tiles_used, 1)

            products(0)
            with pe.Fori(1, DIAG_IT) as it:
                products(it)
            pe.wait_ge(diag_done, 2)
            for b in range(BC):
                for c in range(NCH):
                    bank, rows = sums_of(c)
                    s = c * BC + b
                    mm(ps[rows, bank, b * P:(b + 1) * P], mask_diag_h[:, s, :], ident[:, :])
                for c in range(NCH):
                    bank, rows = sums_of(c)
                    s = c * BC + b
                    last = mm(ps[rows, Q + bank, b * P:(b + 1) * P], adj_diag_h[:, s, :], ident[:, :])
            last.then_inc(sums_done, 1)
            with pe.Fori(DIAG_IT, S // 2) as it:
                products(it)

            pe.wait_ge(moved_a, 2)
            pe.wait_ge(counts_step, S * Q)
            for s in range(S):
                last = mm(ps[:, 5, 2 * S + s:2 * S + s + 1], counts[:, s * P:(s + 1) * P], ones[:, 0:1], True, True)
            last.then_inc(degrees, 1)

            def score(c):
                for s in range(c * BC, (c + 1) * BC):
                    last = mm(ps[:, 4, 2 * s:2 * s + 2], X1[0:F, s * P:(s + 1) * P], score_w[0:F, :], True, True)
                return last

            pe.wait_ge(moved_a, 4)
            for c in range(2):
                pe.wait_ge(moved, c + 1)
                score(c)
            pe.wait_ge(flag_step, 4)
            mm(ps[0:1, 5, 0:1], excess[:, 2:3], ones_f[:, :], True, True).then_inc(excess_sum, 1)
            pe.wait_ge(flag_step, 6)
            mm(ps[0:1, 5, 1:2], longest[:, 0:1], ones_f[:, :], True, True).then_inc(excess_sum, 1)
            pe.wait_ge(moved_a, NCH)
            for c in range(NCH):
                if c >= 2:
                    pe.wait_ge(room_ready, c - 1)
                mm(ps[:, 6 + c % 2, :], later[:, :], counts[:, chunk(c)], True, True).then_inc(behind, 1)
                if c >= 2:
                    pe.wait_ge(moved, c + 1)
                    last = score(c)
            last.then_inc(scores, 1)

            def negative_products(s, first):
                pe.wait_ge(neg_v, s * 10 + 11)
                for q in range(Q):
                    for part in range(PARTS):
                        for c in range(2):
                            at = (2 * q + c) * BANK
                            mm(ps[c * F:(c + 1) * F, q, :], stage_b[:, 0, part * F:(part + 1) * F],
                               masks[:, at:at + BANK], first and part == 0)
                    for c in range(2):
                        at = (2 * q + c) * BANK
                        last = mm(ps[c * F:(c + 1) * F, Q + q, :], stage_f[:, 0, :], tiles[:, at:at + BANK], first)
                last.then_inc(neg_used, 1)

            has_neg = load_flag(pe, "pe_neg", 0)
            with pe.If_ne(has_neg, 0):
                pe.wait_ge(room_ready, NCH)
                pe.wait_ge(scores, 1)
                pe.nop().then_inc(neg_used, 1)
                negative_products(0, True)
                with pe.Fori(1, S) as s:
                    negative_products(s, False)
                pe.wait_ge(neg_out, 3 * NCH)
                for s in range(S):
                    mm(ps[:, 0, 2 * s:2 * s + 2], Yn[:, s * P:(s + 1) * P], score_w[F:P, :], True, True)
                    last = mm(ps[:, 0, 2 * S + s:2 * S + s + 1], counts[:, s * P:(s + 1) * P], ones[:, 0:1], True, True)
                last.then_inc(neg_scores, 1)
                pe.wait_ge(neg_out, 3 * NCH + 3)
                for c in range(NCH):
                    last = score(c)
                last.then_inc(neg_scores, 1)

            pe.wait_ge(moved, NCH)
            for c in range(NCH):
                bank, rows = sums_of(c)
                for b in range(BC):
                    last = mm(ps[rows, bank, b * P:(b + 1) * P], h[:, c * BC + b, :], ident[:, :], True, True)
                last.then_inc(turned, 1)

            def spread_weights(w, c, done):
                bank, rows = sums_of(c)
                for b in range(BC):
                    s = c * BC + b
                    last = mm(ps[rows, bank, b * P:(b + 1) * P], w[:, s:s + 1].to_broadcast((P, F)),
                              ident[:, :], True, True)
                last.then_inc(done, 1)

            def mix(c):
                pe.wait_ge(turned_out, c // 2 * 2 + 2)
                spread_weights(pp, c, spread)
                with pe.If_ne(has_neg, 0):
                    pe.wait_ge(mixed, c + 1)
                    spread_weights(pm, c, neg_spread)
                    pe.wait_ge(neg_mixed, 2 * c + 2)

            def cells(g):
                par = g % 2
                if g >= 2:
                    pe.wait_ge(gru_v, (g - 2) * GV + 2)
                for b in range(2):
                    s = 2 * g + b
                    bank = 6 - 2 * par + b
                    mm(ps[:, bank, :], ones[0:PARTS, :], bias_rows[:, :], True)
                    with pe.If_ne(has_neg, 0):
                        mm(ps[:, bank, 0:G], Yn[:, s * P:(s + 1) * P], gate_w[F:P, :]).then_inc(neg_gates, 1)
                        pe.wait_ge(neg_gates, s + 1)
                    mm(ps[:, bank, :], X1[:, s * P:(s + 1) * P], gru_w[:, :])
                    last = mm(ps[:, bank, NODE:HID], Y[:, s * P:(s + 1) * P], gate_w[0:F, :], False, True)
                last.then_inc(gru_pe, 1)

            def decayed(g, odd):
                for half in range(2):
                    pe.wait_ge(weighed, 4 * g + 2 * odd + half + 1)
                    place = weights(g, odd, half)
                    for q in range(2):
                        for part in range(PARTS):
                            for c in range(2):
                                at = (2 * q + c) * BANK
                                last = mm(ps[c * F:(c + 1) * F, 2 * half + q, :],
                                          stage_b[:, 2 * (g % 2) + odd, part * F:(part + 1) * F],
                                          place[:, at:at + BANK].bitcast(BF16), (g, odd, part) == (0, 0, 0))
                    last.then_inc(weights_used, 1)

            pe.wait_ge(bias_moved, 16)
            pe.wait_ge(gru_w_loaded, 16 * 10)
            pe.wait_ge(att_final, 1)
            for c in range(2):
                mix(c)
            pe.wait_ge(mixed, 1)
            for g in range(2):
                cells(g)
            for c in range(2, NCH):
                mix(c)
            pe.wait_ge(mixed, NCH)
            cells(2)
            for g in range(GROUPS):
                pe.wait_ge(gru_p, GP * (g + 1))
                decayed(g, 0)
                if g + 3 < GROUPS:
                    cells(g + 3)
                decayed(g, 1)
            for q in range(Q):
                pe.wait_ge(wh_out, NCH)
                for b in range(S // Q):
                    s = q * (S // Q) + b
                    last = mm(ps[:, Q + q, b * F:(b + 1) * F], WH[:, s * P:(s + 1) * P], w1_s[:, :], True, True)
                last.then_inc(projected, 1)


_ORDER = ["adj", "adj_diag", "x", "WT", "a2", "wie", "wie_neg", "whe", "win", "whn", "bie", "bhe", "bin", "bhn", "w1", "b1"]


def kernel(**inputs):
    import numpy as _np
    import concourse.bacc as _bacc
    from concourse import mybir as _mybir
    from concourse.bass_utils import run_bass_kernel_spmd as _run

    v = {k: _np.asarray(a) for k, a in inputs.items()}
    L = "L0_gnn_"
    sent = {
        "adj": v["adj"].reshape(P, S, P, S)[:, ::-1, :, ::-1].transpose(2, 3, 1, 0).reshape(P, S * N),
        "adj_diag": v["adj"].diagonal().reshape(P, S)[:, ::-1],
        "x": v["x"].reshape(P, S, F)[:, ::-1],
        "WT": v[L + "W_gat"].T,
        "a2": v[L + "a_gat"].reshape(2, F).T,
        "wie": v[L + "w_ih_e"].T[0:F],
        "wie_neg": v[L + "w_ih_e"].T[F:2 * F],
        "whe": v[L + "w_hh_e"].T,
        "win": v[L + "w_ih_n"].T,
        "whn": v[L + "w_hh_n"].T,
        "bie": v[L + "b_ih_e"],
        "bhe": v[L + "b_hh_e"],
        "bin": v[L + "b_ih_n"],
        "bhn": v[L + "b_hh_n"],
        "w1": v["L1_gnn_weight"],
        "b1": v["L1_gnn_bias"],
    }
    nc = _bacc.Bacc("TRN2", target_bir_lowering=False, num_devices=1)
    arrays, args = {}, []
    for name in _ORDER:
        a = _np.ascontiguousarray(sent[name])
        arrays[f"in_{name}"] = a
        args.append(nc.dram_tensor(f"in_{name}", a.shape, _mybir.dt.from_np(a.dtype), kind="ExternalInput").ap())
    args.append(nc.dram_tensor("out_0", (P, S, F), F32, kind="ExternalOutput").ap())
    graph_layers(nc, *args)
    r = _run(nc, [arrays], core_ids=[0])
    return r.results[0]["out_0"][:, ::-1].reshape(N, F)
```

```python
from contextlib import ExitStack

import concourse.bass as bass
from concourse import mybir

F32 = mybir.dt.float32
BF16 = mybir.dt.bfloat16
I8 = mybir.dt.int8
U8 = mybir.dt.uint8
I16 = mybir.dt.int16
U16 = mybir.dt.uint16
I32 = mybir.dt.int32
ALU = mybir.AluOpType
ACT = mybir.ActivationFunctionType
AX_X = mybir.AxisListType.X

P = 128
N = 4096
F = 64
S = N // P
TW = N // 2
BANK = 512
NCH = N // BANK
BC = BANK // P
Q = 4
RING = 4
PARTS = 3
G = 3 * F
RZ = 2 * F
NODE, HID = G, 2 * G
WA = 2 * G + 2 * F
GROUPS = S // 2
ALPHA = 0.2
NEG_INF = -9.0e15
MAX_NEIGH = 100
UNIT = 128
FLAG = 128
LEAD = 4
SCALE = 2.0 ** (127 - MAX_NEIGH)
EPS = 1e-5
EARLY_IT = 8

GV, GA, GP = 13, 2, 9
ATT_EXP = 23


def graph_layers(nc, adj, adj_diag, x, WT, a2, wie, wie_neg, whe, win, whn, bie, bhe, bin_, bhn, w1, b1, out):
    assert MAX_NEIGH + 1 < FLAG - 1
    with ExitStack() as ctx:
        def sb(name, shape, dt):
            return ctx.enter_context(nc.sbuf_tensor(name, shape, dt))

        def sem(name):
            return ctx.enter_context(nc.semaphore(name))

        ps = ctx.enter_context(nc.psum_tensor("ps", [P, 8, BANK], F32))
        signs = sb("signs", [P, S * N], I8)
        tiles = sb("tiles", [P, RING * TW], F32)
        counts = sb("counts", [P, N], BF16)
        xs = sb("xs", [P, S, F], F32)
        h = sb("h", [P, S, F], F32)
        masks = sb("masks", [P, N], BF16)
        stage_f = sb("stage_f", [P, 2, F], F32)
        stage_b = sb("stage_b", [P, 4, G], BF16)
        ident = sb("ident", [P, P], F32)
        later = sb("later", [P, P], BF16)
        ones = sb("ones", [P, P], BF16)
        gru_w = sb("gru_w", [P, WA], F32)
        gate_w = sb("gate_w", [P, G], F32)
        score_w = sb("score_w", [P, 2], F32)
        w1_s = sb("w1_s", [F, F], F32)
        bias_rows = sb("bias_rows", [PARTS, WA], BF16)
        bias_1 = sb("bias_1", [P, F], F32)
        diag = sb("diag", [P, S], F32)
        sign_sum = sb("sign_sum", [P, 2 * S], F32)
        offdiag = sb("offdiag", [P, P], BF16)
        stat = sb("stat", [P, 16, S], F32)
        full_room = sb("full_room", [P, 1], F32)
        done_mark = sb("done_mark", [1, 1], F32)
        flag_off = sb("flag_off", [P, 1], F32)
        ones_f = sb("ones_f", [P, 1], F32)
        excess = sb("excess", [P, 3], F32)
        flag = sb("flag", [1, 2], I32)
        longest = sb("longest", [P, 2], F32)
        rest = sb("rest", [P, RZ], F32)
        consts_t = sb("consts_t", [P, 4, 2], F32)
        rz_t = sb("rz_t", [P, 4 * RZ], F32)
        nn_t = sb("nn_t", [P, 4 * F], F32)
        dd_t = sb("dd_t", [P, 4 * F], F32)
        moments = sb("moments", [P, 2, 6], F32)
        mean_var = sb("mean_var", [P, 2, 2], F32)
        rs_nm = sb("rs_nm", [P, 2, 2], F32)
        kept_sums = nc.dram_tensor("kept_sums", (F, N), F32).ap()
        kept_room = nc.dram_tensor("kept_room", (P, N), U8).ap()

        def slots(ap):
            return ap.rearrange("p (s f) -> p s f", s=S)

        def early(slot, n):
            return signs[:, slot * N:slot * N + n * 4].bitcast(F32)

        bias_in = early(S - 12, 4 * G)[0:1, :]
        bias_all = early(S - 13, WA)[0:1, :]
        bias_parts = signs[0:1, (S - 14) * N:(S - 14) * N + 2 * PARTS * WA].bitcast(BF16)
        wt_s = early(S - 15, F)[0:F, :]
        a2_s = signs[0:F, (S - 15) * N + 512:(S - 15) * N + 520].bitcast(F32)
        win_s = signs[0:F, (S - 15) * N + 1024:(S - 15) * N + 1024 + 4 * G].bitcast(F32)
        X1 = tiles[:, 0:N]
        Y = tiles[0:F, N:2 * N]
        Yn = tiles[F:P, N:2 * N]
        AN = counts[:, :].bitcast(F32)
        WH = tiles[0:F, 0:N]
        room = masks[:, 0:N // 2].bitcast(U8)
        room_pairs = masks[:, 0:N // 2].bitcast(U16)
        codes = signs[:, :].bitcast(U8)
        pairs = signs[:, :].bitcast(U16)
        rz = rz_t[:, :].rearrange("p (b c f) -> p b c f", b=2, c=2)
        nn = nn_t[:, :].rearrange("p (b c f) -> p b c f", b=2, c=2)
        dd = dd_t[:, :].rearrange("p (b c f) -> p b c f", b=2, c=2)
        ss = rz_t[:, 0:RZ].rearrange("p (b f) -> p b f", b=2)
        added, x1_t = (nn_t[:, n * RZ:(n + 1) * RZ].rearrange("p (b f) -> p b f", b=2) for n in range(2))
        h2 = masks[:, N // 2:N // 2 + 2 * RZ].bitcast(F32)
        c_eps, c_half, c_scale, c_neg = (consts_t[:, n, :] for n in range(4))
        (term, nz_d, npos, has, ep, mx, en, e0, zz, pp, deg, nneg, n_zero, pm) = (
            stat[:, n, :] for n in range(14))
        neg_score = stat[:, 14:16, :].rearrange("p e s -> p (e s)").rearrange("p (s e) -> p s e", e=2)

        names = """diag_loaded w_loaded gru_w_loaded bias_loaded bias_moved consts bias_step
            counts_clear prep rstd_step h_ready own_step small_w small_w_out counts_step masks_made signs_kept
            masks_used tiles_used staged moved moved_a turned turned_out scores att att_exp
            att_final spread mixed behind room_ready gru_pe gru_v gru_a gru_p marked coded room_step
            weighed weights_used bias_added wh_out projected final stored degrees flag_step excess_sum
            flag_ready neg_saved neg_loaded neg_v neg_used neg_reloaded neg_out neg_scores neg_spread
            neg_mixed neg_gates long_step
            normed_x1""".split()
        (diag_loaded, w_loaded, gru_w_loaded, bias_loaded, bias_moved, consts, bias_step,
         counts_clear, prep, rstd_step, h_ready, own_step, small_w, small_w_out, counts_step, masks_made, signs_kept,
         masks_used, tiles_used, staged, moved, moved_a, turned, turned_out, scores, att, att_exp,
         att_final, spread, mixed, behind, room_ready, gru_pe, gru_v, gru_a, gru_p, marked, coded, room_step,
         weighed, weights_used, bias_added, wh_out, projected, final, stored, degrees, flag_step, excess_sum,
         flag_ready, neg_saved, neg_loaded, neg_v, neg_used, neg_reloaded, neg_out, neg_scores, neg_spread,
         neg_mixed, neg_gates, long_step,
         normed_x1) = map(sem, names)
        x_loaded = [sem(f"x_loaded{c}") for c in range(2)]
        tile_loaded = [sem(f"tile_loaded{u}") for u in range(RING)]
        N_CONST = 17

        def load_flag(eng, name, n):
            reg = eng.alloc_register(name)
            eng.wait_ge(flag_ready, 1)
            eng.reg_load(reg, flag[0:1, n:n + 1])
            return reg

        def weights(g, odd, half):
            aside = odd and not (isinstance(g, int) and g == 0)
            ring = (signs[:, 0:2 * N] if aside else counts[:, :]).bitcast(I16)
            return ring[:, half * TW:(half + 1) * TW]

        def sums_of(c):
            return c // 2, slice(F * (c % 2), F * (c % 2) + F)

        def chunk(c):
            return slice(c * BANK, (c + 1) * BANK)

        block = ctx.enter_context(nc.Block())

        @block.sync
        def _(sp):
            sp.dma_start(xs[:, 0:2, :], x[:, 0:2, :]).then_inc(x_loaded[0], 16)
            for u in range(RING):
                sp.dma_start(tiles[:, u * TW:(u + 1) * TW], adj[:, u * TW:(u + 1) * TW]).then_inc(tile_loaded[u], 16)
                if u == 0:
                    sp.dma_start(xs[:, 2:S, :], x[:, 2:S, :]).then_inc(x_loaded[1], 16)
            sp.dma_start(diag[:, :], adj_diag).then_inc(diag_loaded, 16)
            for n, b in enumerate((bie, bhe, bin_, bhn)):
                sp.dma_start(bias_in[:, n * G:(n + 1) * G], b.rearrange("(a n) -> a n", a=1)).then_inc(bias_loaded, 16)
            sp.wait_ge(consts, N_CONST)
            for dst, src in ((gru_w[0:F, 0:F], wie[:, RZ:G]), (gru_w[0:F, F:G], wie[:, 0:RZ]),
                             (gru_w[F:P, F:G], whe[:, 0:RZ]), (gru_w[F:P, HID:HID + F], whe[:, RZ:G]),
                             (gru_w[F:P, NODE + F:HID], whn[:, 0:RZ]), (gru_w[F:P, HID + F:WA], whn[:, RZ:G]),
                             (gate_w[F:P, 0:F], wie_neg[:, RZ:G]), (gate_w[F:P, F:G], wie_neg[:, 0:RZ]),
                             (w1_s[:, :], w1), (bias_1[:, :], bass.AP(tensor=b1.tensor, offset=0, ap=[[0, P], [1, F]]))):
                sp.dma_start(dst, src).then_inc(gru_w_loaded, 16)
            with sp.Fori(1, S // 2) as it:
                for u in range(RING):
                    sp.wait_ge(tiles_used, it * RING + (u + 1 - RING))
                    sp.wait_ge(masks_made, it * RING + (u + 1 - RING))
                    sp.wait_ge(signs_kept, it * RING + (u + 1 - RING))
                    sp.dma_start(tiles[:, u * TW:(u + 1) * TW],
                                 adj[:, bass.ds(it * (2 * N) + u * TW, TW)]).then_inc(tile_loaded[u], 16)

            has_neg = load_flag(sp, "sp_neg", 0)
            with sp.If_ne(has_neg, 0):
                sp.wait_ge(moved, NCH)
                sp.wait_ge(room_ready, NCH)
                sp.dma_start(kept_sums, X1[0:F, :]).then_inc(neg_saved, 16)
                sp.dma_start(kept_room, room).then_inc(neg_saved, 16)
                sp.wait_ge(neg_saved, 32)
                with sp.Fori(0, S) as s:
                    sp.wait_ge(neg_used, s + 1)
                    sp.dma_start(tiles[:, 0:N], adj[:, bass.ds(s * N, N)]).then_inc(neg_loaded, 16)
                sp.wait_ge(neg_used, S + 1)
                sp.dma_start(X1[0:F, :], kept_sums).then_inc(neg_reloaded, 16)
                sp.dma_start(room, kept_room).then_inc(neg_reloaded, 16)

            for q in range(Q):
                part = slice(q * (S // Q), (q + 1) * (S // Q))
                sp.wait_ge(final, q + 1)
                sp.dma_start(out[:, part, :], xs[:, part, :]).then_inc(stored, 16)
            sp.wait_ge(stored, 16 * Q)

        @block.gpsimd
        def _(pool):
            for ap, value in ((c_eps, EPS), (c_half, -0.5), (c_scale, SCALE), (c_neg, -1.0), (ident[:, :], 1.0),
                              (later[:, :], -1.0), (ones[:, :], 1.0), (offdiag[:, :], 1.0),
                              (full_room[:, :], float(MAX_NEIGH + 1)),
                              (flag_off[:, :], -float(UNIT * FLAG)), (gru_w[:, :], 0.0),
                              (ones_f[:, :], 1.0), (nneg, 0.0), (stat[:, 14:16, :], 0.0), (flag[:, :], 0)):
                pool.memset(ap, value).then_inc(consts, 1)
            pool.wait_ge(consts, N_CONST - 3)
            pool.affine_select(out=ident[:, :], in_=ident[:, :], compare_op=ALU.is_equal, fill=0.0, base=0,
                               pattern=[[-1, P]], channel_multiplier=1).then_inc(consts, 1)
            pool.affine_select(out=offdiag[:, :], in_=offdiag[:, :], compare_op=ALU.not_equal, fill=0.0, base=0,
                               pattern=[[-1, P]], channel_multiplier=1).then_inc(consts, 1)
            pool.affine_select(out=later[:, :], in_=later[:, :], compare_op=ALU.is_gt, fill=0.0, base=0,
                               pattern=[[-1, P]], channel_multiplier=1).then_inc(consts, 1)

            def factors(it):
                rs, nm = rs_nm[:, 0, :], rs_nm[:, 1, :]
                pool.wait_ge(prep, it * 4 + 4)
                pool.tensor_tensor(rs, mean_var[:, :, 1], c_eps, ALU.add).then_inc(rstd_step, 1)
                pool.wait_ge(rstd_step, it * 4 + 1)
                pool.tensor_tensor(rs, rs, c_half, ALU.pow).then_inc(rstd_step, 1)
                pool.wait_ge(rstd_step, it * 4 + 2)
                pool.tensor_tensor(nm, mean_var[:, :, 0], rs, ALU.mult).then_inc(rstd_step, 1)
                pool.wait_ge(rstd_step, it * 4 + 3)
                pool.tensor_tensor(nm, nm, c_neg, ALU.mult).then_inc(rstd_step, 1)

            def stage(it):
                for k in range(2):
                    if not (isinstance(it, int) and it == 0):
                        pool.wait_ge(tiles_used, it * RING + (2 * (k + 1) - RING))
                    hs = stage_f[:, k, :]
                    hi, mid, lo = (stage_b[:, k, n * F:(n + 1) * F] for n in range(PARTS))
                    base = it * 10 + 5 * k
                    pool.wait_ge(h_ready, it * 2 + (k + 1))
                    pool.tensor_copy(hs, h[:, bass.ds(it * 2 + k, 1), :].rearrange("p a f -> p (a f)"))\
                        .then_inc(staged, 1)
                    pool.wait_ge(staged, base + 1)
                    pool.tensor_tensor(hi, hs, ones[:, 0:F], ALU.mult).then_inc(staged, 1)
                    pool.wait_ge(staged, base + 2)
                    pool.tensor_tensor(rest[:, 0:F], hs, hi, ALU.subtract).then_inc(staged, 1)
                    pool.wait_ge(staged, base + 3)
                    pool.tensor_tensor(mid, rest[:, 0:F], ones[:, 0:F], ALU.mult).then_inc(staged, 1)
                    pool.wait_ge(staged, base + 4)
                    pool.tensor_tensor(lo, rest[:, 0:F], mid, ALU.subtract).then_inc(staged, 1)

            factors(0)
            stage(0)
            factors(1)
            pool.wait_ge(bias_loaded, 16 * 4)
            be_i, be_h, bn_i, bn_h = (bias_in[:, n * G:(n + 1) * G] for n in range(4))
            for at, bi, bh in ((0, be_i, be_h), (NODE, bn_i, bn_h)):
                pool.tensor_copy(bias_all[:, at:at + F], bi[:, RZ:G]).then_inc(bias_step, 1)
                pool.tensor_tensor(bias_all[:, at + F:at + G], bi[:, 0:RZ], bh[:, 0:RZ], ALU.add).then_inc(bias_step, 1)
            pool.tensor_copy(bias_all[:, HID:HID + F], be_h[:, RZ:G]).then_inc(bias_step, 1)
            pool.tensor_copy(bias_all[:, HID + F:WA], bn_h[:, RZ:G]).then_inc(bias_step, 1)

            def bias_split(part):
                pool.wait_ge(bias_step, 6 + 2 * part)
                piece = bias_parts[:, part * WA:(part + 1) * WA]
                pool.tensor_copy(piece, bias_all[:, :]).then_inc(bias_step, 1)
                if part < PARTS - 1:
                    pool.wait_ge(bias_step, 7 + 2 * part)
                    pool.tensor_tensor(bias_all[:, :], bias_all[:, :], piece, ALU.subtract).then_inc(bias_step, 1)

            stage(1)
            for part in range(PARTS):
                bias_split(part)
                factors(part + 2)
                stage(part + 2)
            with pool.Fori(PARTS + 2, S // 2) as it:
                factors(it)
                stage(it)

            def norm(g, par):
                rs, nm = rs_nm[:, 0, :], rs_nm[:, 1, :]
                hi, mid, lo = (stage_b[:, 2 * par:2 * par + 2, n * F:(n + 1) * F] for n in range(PARTS))
                h2v, rv = (t.rearrange("p (b f) -> p b f", b=2) for t in (h2, rest[:, :]))
                one = ones[:, :].rearrange("p (b f) -> p b f", b=2)

                def after(k):
                    pool.wait_ge(gru_p, g * GP + k)

                pool.wait_ge(gru_v, g * GV + GV)
                pool.tensor_tensor(rs, mean_var[:, :, 1], c_eps, ALU.add).then_inc(gru_p, 1)
                after(1)
                pool.tensor_tensor(rs, rs, c_half, ALU.pow).then_inc(gru_p, 1)
                after(2)
                pool.tensor_tensor(rs, rs, c_scale, ALU.mult).then_inc(gru_p, 1)
                after(3)
                pool.tensor_tensor(nm, mean_var[:, :, 0], rs, ALU.mult).then_inc(gru_p, 1)
                after(4)
                pool.tensor_tensor(nm, nm, c_neg, ALU.mult).then_inc(gru_p, 1)
                pool.wait_ge(normed_x1, g * 2 + 2)
                if not (isinstance(g, int) and g < 2):
                    pool.wait_ge(weights_used, g * 4 - 4)
                pool.tensor_tensor(hi, h2v, one, ALU.mult).then_inc(gru_p, 1)
                after(6)
                pool.tensor_tensor(rv, h2v, hi, ALU.subtract).then_inc(gru_p, 1)
                after(7)
                pool.tensor_tensor(mid, rv, one, ALU.mult).then_inc(gru_p, 1)
                after(8)
                pool.tensor_tensor(lo, rv, mid, ALU.subtract).then_inc(gru_p, 1)

            pool.wait_ge(att_final, 1)
            norm(0, 0)
            norm(1, 1)
            with pool.Fori(1, GROUPS // 2) as it:
                norm(it * 2, 0)
                norm(it * 2 + 1, 1)
            pool.tensor_tensor(xs[:, :, :], xs[:, :, :], bias_1[:, None, :].to_broadcast((P, S, F)), ALU.add)\
                .then_inc(bias_added, 1)

        @block.scalar
        def _(act):
            for dst, src in ((wt_s, WT), (a2_s, a2), (win_s[:, 0:F], win[:, RZ:G]), (win_s[:, F:G], win[:, 0:RZ])):
                act.dma_start(dst, src).then_inc(w_loaded, 16)

            def normed_x(it):
                act.wait_ge(rstd_step, it * 4 + 4)
                for b in range(2):
                    act.activation(h[:, bass.ds(it * 2 + b, 1), :].rearrange("p a f -> p (a f)"),
                                   xs[:, bass.ds(it * 2 + b, 1), :].rearrange("p a f -> p (a f)"), ACT.Relu,
                                   bias=rs_nm[:, 1, b:b + 1], scale=rs_nm[:, 0, b:b + 1]).then_inc(h_ready, 1)

            def keep_signs(it, last=False):
                for u in range(RING):
                    act.wait_ge(tile_loaded[u], it * 16 + 16)
                    act.activation(signs[:, bass.ds(it * (2 * N) + u * TW, TW)], tiles[:, u * TW:(u + 1) * TW],
                                   ACT.Sign, accum_out=sign_sum[:, bass.ds(it * RING + u, 1)]).then_inc(signs_kept, 1)
                    if u == 1 and not last:
                        normed_x(it + 1)

            normed_x(0)
            keep_signs(0)
            with act.Fori(1, EARLY_IT - 1) as it:
                keep_signs(it)
            act.wait_ge(bias_step, 11)
            act.dma_start(bias_rows[:, :], bias_parts.rearrange("a (r n) -> a r n", r=PARTS)).then_inc(bias_moved, 16)
            keep_signs(EARLY_IT - 1)
            act.wait_ge(small_w_out, 3)
            act.wait_ge(bias_moved, 16)
            with act.Fori(EARLY_IT, S // 2 - 1) as it:
                keep_signs(it)
            keep_signs(S // 2 - 1, True)

            act.wait_ge(tiles_used, 2 * S)
            act.wait_ge(masks_made, 2 * S)
            act.wait_ge(signs_kept, 2 * S)
            for c in (2, 3, 0, 1, 6, 7, 4, 5):
                b, rows = sums_of(c)
                act.activation(Y[:, chunk(c)], ps[rows, Q + b, :], ACT.Copy).then_inc(moved_a, 1)
            for c in range(NCH):
                act.wait_ge(behind, c + 1)
                act.activation(room[:, chunk(c)], ps[:, 6 + c % 2, :], ACT.Relu, bias=full_room[:, :])                    .then_inc(room_ready, 1)

            def turn_out(c):
                b, rows = sums_of(c)
                act.wait_ge(turned, c + 1)
                act.activation(X1[F:P, chunk(c)], ps[rows, b, :], ACT.Copy).then_inc(turned_out, 1)

            for c in range(4):
                turn_out(c)
            for e in (ep, en, e0):
                act.wait_ge(att, ATT_EXP)
                act.activation(e, e, ACT.Exp).then_inc(att_exp, 1)
            for c in range(4, NCH):
                turn_out(c)

            def weigh(g, odd, half):
                place = weights(g, odd, half)
                n = g * 4 + (odd * 2 + half)
                act.wait_ge(coded, n + 1)
                if not isinstance(g, int) or g > 1:
                    act.wait_ge(weights_used, n - 3)
                elif g == 1 and odd:
                    act.wait_ge(weighed, 4)
                elif (g, odd) != (0, 0):
                    act.wait_ge(weights_used, n - 1)
                act.activation(place, codes[:, bass.ds(g * (2 * N) + (odd * N + half * TW), TW)], ACT.Relu,
                               bias=flag_off[:, :], scale=float(UNIT)).then_inc(weighed, 1)

            def gates(g, par):
                A = ps[:, 6 - 2 * par:8 - 2 * par, 0:HID].rearrange("p b (c f) -> p b c f", c=2)
                act.wait_ge(gru_pe, g + 1)
                if not (isinstance(g, int) and g == 0):
                    act.wait_ge(gru_v, g * GV - 2)
                act.activation(rz[:, :, :, :], A[:, :, :, F:G], ACT.Sigmoid).then_inc(gru_a, 1)

            def candidates(g):
                act.wait_ge(gru_v, g * GV + 2)
                act.activation(nn[:, :, :, :], nn[:, :, :, :], ACT.Tanh).then_inc(gru_a, 1)

            def normed(g, par):
                act.wait_ge(gru_p, g * GP + 5)
                for b in range(2):
                    act.activation(h2[:, b * F:(b + 1) * F],
                                   xs[:, bass.ds(g * 2 + b, 1), :].rearrange("p a f -> p (a f)"), ACT.Relu,
                                   bias=rs_nm[:, 1, b:b + 1], scale=rs_nm[:, 0, b:b + 1]).then_inc(normed_x1, 1)

            def group(g, par):
                static = isinstance(g, int)
                if not static or g < GROUPS:
                    gates(g, par)
                if not static or g >= 2:
                    weigh(g - 2, 0, 1)
                if not static or g < GROUPS:
                    candidates(g)
                if not static or g >= 2:
                    weigh(g - 2, 1, 0)
                if not static or 1 <= g <= GROUPS:
                    normed(g - 1, 1 - par)
                if not static or g >= 2:
                    weigh(g - 2, 1, 1)
                if not static or 1 <= g <= GROUPS:
                    weigh(g - 1, 0, 0)

            act.wait_ge(att_final, 1)
            act.wait_ge(behind, NCH)
            group(0, 0)
            has_neg = load_flag(act, "act_neg", 0)
            with act.If_ne(has_neg, 0):
                act.wait_ge(neg_mixed, 2 * NCH)
            for g in range(1, 4):
                group(g, g % 2)
            with act.Fori(2, GROUPS // 2) as it:
                group(it * 2, 0)
                group(it * 2 + 1, 1)
            group(GROUPS, 0)
            group(GROUPS + 1, 1)
            for c in range(0, NCH, 2):
                act.wait_ge(weights_used, 2 * S - 1 + c // 4)
                act.activation(WH[:, chunk(c)], ps[0:F, c // 2, :], ACT.Copy).then_inc(wh_out, 1)

        @block.vector
        def _(dve):
            seen = {}

            def link(ins, s):
                seen[s.name] = seen.get(s.name, 0) + 1
                ins.then_inc(s, 1)
                dve.wait_ge(s, seen[s.name])
                return seen[s.name]

            def stats(it):
                for b in range(2):
                    dve.bn_stats(moments[:, b, :], xs[:, bass.ds(it * 2 + b, 1), :].rearrange("p a f -> p (a f)"))                        .then_inc(prep, 1)

            def aggregate():
                for b in range(2):
                    dve.bn_aggr(mean_var[:, b, :], moments[:, b, :]).then_inc(prep, 1)

            def mark(n):
                dve.wait_ge(signs_kept, n + 1)
                kept = pairs[:, bass.ds(n * (TW // 2), TW // 2)]
                dve.tensor_scalar(kept, kept, float(FLAG - 1), None, ALU.mult).then_inc(marked, 1)

            def make_masks(it, own_half, last=False):
                first = isinstance(it, int) and it == 0
                for u in range(RING):
                    k, half = divmod(u, 2)
                    mask = masks[:, half * TW:(half + 1) * TW]
                    count = counts[:, half * TW:(half + 1) * TW]
                    dve.wait_ge(tile_loaded[u], it * 16 + 16)
                    if not (first and k == 0):
                        dve.wait_ge(masks_used, it * RING + (u - 1))
                        dve.wait_ge(counts_step, it * RING + (u - 1))
                    if u == 0:
                        dve.wait_ge(prep, it * 4 + 4)
                    dve.tensor_scalar(mask, tiles[:, u * TW:(u + 1) * TW], 0.0, None, ALU.not_equal)                        .then_inc(masks_made, 1)
                    if u == 0 and not last:
                        if first:
                            dve.wait_ge(x_loaded[1], 16)
                        stats(it + 1)
                    if not (first and u == 0):
                        mark(it * RING + (u - 1))
                    dve.wait_ge(masks_made, it * RING + (u + 1))
                    if u == 0 and not last:
                        dve.wait_ge(prep, it * 4 + 6)
                        dve.wait_ge(rstd_step, it * 4 + 4)
                    dve.tensor_tensor(count, count, mask, ALU.add).then_inc(counts_step, 1)
                    if u == 0 and not last:
                        aggregate()
                    if first and u == 0:
                        dve.wait_ge(small_w, 1)
                        dve.tensor_copy(gate_w[0:F, :], ps[0:F, 7, 0:G]).then_inc(small_w_out, 1)
                        for f in (0, F):
                            dve.tensor_copy(score_w[f:f + F, :], ps[0:F, 7, G:G + 2]).then_inc(small_w_out, 1)
                    if half == own_half:
                        own = bass.ds(it * (2 * P) + k * P, P)
                        dve.wait_ge(counts_step, it * RING + (u + 1))
                        dve.tensor_tensor(masks[:, own], masks[:, own], offdiag[:, :], ALU.mult).then_inc(own_step, 1)
                        own = bass.ds(it * (2 * P) + k * (N + P), P)
                        dve.wait_ge(signs_kept, it * RING + (u + 1))
                        dve.tensor_tensor(tiles[:, own], tiles[:, own], offdiag[:, :], ALU.mult).then_inc(own_step, 1)

            dve.wait_ge(x_loaded[0], 16)
            stats(0)
            dve.wait_ge(prep, 2)
            dve.memset(done_mark[:, :], 0.0)
            aggregate()
            dve.memset(counts[:, :].bitcast(F32), 0.0).then_inc(counts_clear, 1)
            dve.wait_ge(consts, N_CONST)
            dve.wait_ge(counts_clear, 1)
            make_masks(0, 0)
            with dve.Fori(1, S // 4) as it:
                make_masks(it, 0)
            with dve.Fori(S // 4, S // 2 - 1) as it:
                make_masks(it, 1)
            make_masks(S // 2 - 1, 1, True)

            dve.wait_ge(tiles_used, 2 * S)
            dve.wait_ge(masks_made, 2 * S)
            dve.wait_ge(signs_kept, 2 * S)
            def move(c):
                b, rows = sums_of(c)
                dve.tensor_copy(X1[0:F, chunk(c)], ps[rows, b, :]).then_inc(moved, 1)

            for c in range(3):
                move(c)
            mark(2 * S - 1)

            dve.wait_ge(degrees, 1)
            dve.wait_ge(consts, N_CONST)
            link(dve.tensor_copy(deg, ps[:, 5, 2 * S:3 * S]), flag_step)
            link(dve.tensor_reduce(excess[:, 0:1], deg, AX_X, ALU.add), flag_step)
            link(dve.tensor_reduce(excess[:, 1:2], sign_sum[:, :], AX_X, ALU.add), flag_step)
            link(dve.tensor_tensor(excess[:, 2:3], excess[:, 0:1], excess[:, 1:2], ALU.subtract), flag_step)
            link(dve.tensor_scalar(has, deg, float(MAX_NEIGH), None, ALU.is_gt), flag_step)
            link(dve.tensor_reduce(longest[:, 0:1], has, AX_X, ALU.add), flag_step)
            for c in range(3, NCH):
                move(c)
            dve.wait_ge(excess_sum, 2)
            dve.tensor_copy(flag[:, :], ps[0:1, 5, 0:2]).then_inc(flag_ready, 1)

            has_neg = load_flag(dve, "dve_neg", 0)
            has_long = load_flag(dve, "dve_long", 1)
            with dve.If_ne(has_neg, 0):
                dve.wait_ge(neg_saved, 32)
                dve.memset(counts[:, :], 0.0).then_inc(neg_v, 1)
                dve.wait_ge(neg_v, 1)
                with dve.Fori(0, S) as s:
                    dve.wait_ge(neg_loaded, s * 16 + 16)
                    dve.wait_ge(neg_used, s + 1)
                    hs = h[:, bass.ds(s, 1), :].rearrange("p a f -> p (a f)")
                    own = tiles[:, bass.ds(s * P, P)]
                    dve.tensor_scalar(signs[:, bass.ds(s * N, N)], tiles[:, 0:N], 0.0, float(FLAG - 1),
                                      ALU.not_equal, ALU.mult).then_inc(neg_v, 1)
                    dve.wait_ge(neg_v, s * 10 + 2)
                    dve.tensor_scalar(stage_f[:, 0, :], hs, 1.0, None, ALU.mult).then_inc(neg_v, 1)
                    dve.tensor_scalar(stage_b[:, 0, 0:F], hs, 1.0, None, ALU.mult).then_inc(neg_v, 1)
                    dve.scalar_tensor_tensor(out=own, in0=ident[:, :], scalar=0.0, in1=own, op0=ALU.is_equal,
                                             op1=ALU.mult).then_inc(neg_v, 1)
                    dve.wait_ge(neg_v, s * 10 + 5)
                    dve.tensor_tensor(stage_f[:, 1, :], stage_f[:, 0, :], stage_b[:, 0, 0:F], ALU.subtract)                        .then_inc(neg_v, 1)
                    dve.wait_ge(neg_v, s * 10 + 6)
                    dve.tensor_scalar(stage_b[:, 0, F:2 * F], stage_f[:, 1, :], 1.0, None, ALU.mult).then_inc(neg_v, 1)
                    dve.wait_ge(neg_v, s * 10 + 7)
                    dve.tensor_tensor(stage_b[:, 0, 2 * F:G], stage_f[:, 1, :], stage_b[:, 0, F:2 * F], ALU.subtract)                        .then_inc(neg_v, 1)
                    dve.tensor_scalar(masks[:, :], tiles[:, 0:N], 0.0, None, ALU.is_lt).then_inc(neg_v, 1)
                    dve.wait_ge(neg_v, s * 10 + 9)
                    dve.tensor_scalar(tiles[:, 0:N], tiles[:, 0:N], 0.0, None, ALU.min).then_inc(neg_v, 1)
                    dve.tensor_tensor(counts[:, :], counts[:, :], masks[:, :], ALU.add).then_inc(neg_v, 1)
                    dve.wait_ge(neg_v, s * 10 + 11)
                dve.wait_ge(neg_used, S + 1)
                dve.wait_ge(neg_reloaded, 32)
                dve.wait_ge(moved_a, NCH)
                for c in range(NCH):
                    b, rows = sums_of(c)
                    at = chunk(c)
                    dve.tensor_copy(Yn[:, at], ps[rows, b, :]).then_inc(neg_out, 1)
                    dve.tensor_tensor(X1[0:F, at], X1[0:F, at], ps[rows, b, :], ALU.subtract).then_inc(neg_out, 1)
                    dve.tensor_tensor(Y[:, at], Y[:, at], ps[rows, Q + b, :], ALU.subtract).then_inc(neg_out, 1)
                dve.wait_ge(neg_out, 3 * NCH)
                dve.wait_ge(neg_scores, 1)
                dve.tensor_copy(neg_score, ps[:, 0, 0:2 * S].rearrange("p (s e) -> p s e", e=2)).then_inc(neg_out, 1)
                dve.tensor_copy(nneg, ps[:, 0, 2 * S:3 * S]).then_inc(neg_out, 1)
                dve.tensor_copy(AN, ps[:, Q:2 * Q, :].rearrange("p b n -> p (b n)")).then_inc(neg_out, 1)
                dve.wait_ge(neg_out, 3 * NCH + 3)
                dve.wait_ge(neg_scores, 2)

            def code(slot):
                for v in range(2):
                    if not (isinstance(slot, int) and slot == 0):
                        dve.wait_ge(room_step, slot * 2 + (v - 1))
                    half = pairs[:, bass.ds(slot * (N // 2) + v * (TW // 2), TW // 2)]
                    dve.tensor_tensor(half, room_pairs[:, v * (TW // 2):(v + 1) * (TW // 2)], half, ALU.add)                        .then_inc(coded, 1)
                for v in range(2):
                    dve.wait_ge(coded, slot * 2 + (v + 1))
                    half = pairs[:, bass.ds(slot * (N // 2) + v * (TW // 2), TW // 2)]
                    dve.tensor_scalar(room_pairs[:, v * (TW // 2):(v + 1) * (TW // 2)], half,
                                      (FLAG - 1) * 257, None, ALU.bitwise_and).then_inc(room_step, 1)
                with dve.If_ne(has_long, 0):
                    dve.wait_ge(room_step, slot * 2 + 2)
                    dve.scalar_tensor_tensor(out=room, in0=room, scalar=float(FLAG - 1), in1=room,
                                             op0=ALU.not_equal, op1=ALU.mult).then_inc(long_step, 1)
                    dve.wait_ge(long_step, slot + 1)
                    dve.memset(done_mark[:, :], 0.0)

            dve.wait_ge(room_ready, NCH)
            for slot in range(2):
                code(slot)

            dve.wait_ge(scores, 1)
            E = ps[:, 4, 0:2 * S].rearrange("p (s e) -> p s e", e=2)
            dve.wait_ge(diag_loaded, 16)
            link(dve.tensor_scalar(nz_d, diag[:, :], 0.0, -1.0, ALU.not_equal, ALU.mult), att)
            link(dve.tensor_tensor(npos, deg, nz_d, ALU.add), att)
            link(dve.tensor_scalar(n_zero, npos, -1.0, float(N), ALU.mult, ALU.add), att)
            link(dve.tensor_tensor(npos, npos, nneg, ALU.subtract), att)
            for e, own, other, many in ((ep, 0, 1, npos), (en, 1, 0, nneg)):
                link(dve.tensor_tensor(e, E[:, :, own], neg_score[:, :, other], ALU.add), att)
                link(dve.tensor_scalar(term, e, ALPHA, None, ALU.mult), att)
                link(dve.tensor_tensor(e, e, term, ALU.max), att)
                link(dve.tensor_scalar(has, many, 0.5, None, ALU.is_ge), att)
                link(dve.tensor_tensor(e, e, has, ALU.mult), att)
                link(dve.tensor_scalar(has, has, 1.0, -NEG_INF, ALU.subtract, ALU.mult), att)
                link(dve.tensor_tensor(e, e, has, ALU.add), att)
            link(dve.tensor_tensor(mx, ep, en, ALU.max), att)
            link(dve.tensor_scalar(mx, mx, NEG_INF, None, ALU.max), att)
            link(dve.tensor_tensor(ep, ep, mx, ALU.subtract), att)
            link(dve.tensor_tensor(en, en, mx, ALU.subtract), att)
            n = link(dve.tensor_scalar(e0, mx, -1.0, NEG_INF, ALU.mult, ALU.add), att)
            assert n == ATT_EXP

            code(2)
            dve.wait_ge(att_exp, 3)
            link(dve.tensor_tensor(zz, ep, npos, ALU.mult), att)
            link(dve.tensor_tensor(term, en, nneg, ALU.mult), att)
            link(dve.tensor_tensor(zz, zz, term, ALU.add), att)
            link(dve.tensor_tensor(e0, e0, n_zero, ALU.mult), att)
            link(dve.tensor_tensor(zz, zz, e0, ALU.add), att)
            link(dve.reciprocal(zz, zz), att)
            link(dve.tensor_tensor(pp, ep, zz, ALU.mult), att)
            dve.tensor_tensor(pm, en, zz, ALU.mult).then_inc(att_final, 1)
            def mix(c):
                b, rows = sums_of(c)
                at = chunk(c)
                dve.wait_ge(spread, c + 1)
                dve.tensor_tensor(Y[:, at], Y[:, at], ps[rows, b, :], ALU.mult).then_inc(mixed, 1)
                with dve.If_ne(has_neg, 0):
                    dve.wait_ge(mixed, c + 1)
                    dve.wait_ge(neg_spread, c + 1)
                    dve.tensor_tensor(ps[rows, b, :], AN[rows, b * BANK:(b + 1) * BANK], ps[rows, b, :], ALU.mult)                        .then_inc(neg_mixed, 1)
                    dve.wait_ge(neg_mixed, 2 * c + 1)
                    dve.tensor_tensor(Y[:, at], Y[:, at], ps[rows, b, :], ALU.add).then_inc(neg_mixed, 1)
                    dve.wait_ge(neg_mixed, 2 * c + 2)

            def candidates(g, par):
                A = ps[:, 6 - 2 * par:8 - 2 * par, :]
                ins = A[:, :, 0:HID].rearrange("p b (c f) -> p b c f", c=2)[:, :, :, 0:F]
                hid = A[:, :, HID:WA].rearrange("p b (c f) -> p b c f", c=2)
                dve.wait_ge(gru_a, g * GA + 1)
                dve.tensor_tensor(nn[:, :, :, :], rz[:, :, :, 0:F], hid, ALU.mult).then_inc(gru_v, 1)
                dve.wait_ge(gru_v, g * GV + 1)
                dve.tensor_tensor(nn[:, :, :, :], nn[:, :, :, :], ins, ALU.add).then_inc(gru_v, 1)

            def states(g):
                hk = h[:, bass.ds(g * 2, 2), :][:, :, None, :].to_broadcast((P, 2, 2, F))
                dve.wait_ge(gru_a, g * GA + 2)
                dve.tensor_tensor(dd[:, :, :, :], hk, nn[:, :, :, :], ALU.subtract).then_inc(gru_v, 1)
                dve.wait_ge(gru_v, g * GV + 3)
                dve.tensor_tensor(dd[:, :, :, :], dd[:, :, :, :], rz[:, :, :, F:RZ], ALU.mult).then_inc(gru_v, 1)
                dve.wait_ge(gru_v, g * GV + 4)
                dve.tensor_tensor(dd[:, :, :, :], dd[:, :, :, :], nn[:, :, :, :], ALU.add).then_inc(gru_v, 1)
                dve.wait_ge(gru_v, g * GV + 5)
                dve.tensor_tensor(ss, dd[:, :, 0, :], dd[:, :, 1, :], ALU.add).then_inc(gru_v, 1)
                dve.wait_ge(gru_v, g * GV + 6)
                xk = xs[:, bass.ds(g * 2, 2), :]
                dk = diag[:, bass.ds(g * 2, 2)][:, :, None].to_broadcast((P, 2, F))
                dve.tensor_tensor(added, ss, dk, ALU.mult).then_inc(gru_v, 1)
                dve.wait_ge(gru_v, g * GV + 7)
                dve.tensor_tensor(x1_t, added, xk, ALU.add).then_inc(gru_v, 1)
                for b in range(2):
                    dve.wait_ge(gru_v, g * GV + 8)
                    dve.bn_stats(moments[:, b, :], x1_t[:, b, :]).then_inc(gru_v, 1)
                if not (isinstance(g, int) and g == 0):
                    dve.wait_ge(gru_p, g * GP - 5)
                dve.wait_ge(gru_v, g * GV + 10)
                dve.tensor_tensor(xk, added, xk, ALU.add).then_inc(gru_v, 1)
                for b in range(2):
                    dve.bn_aggr(mean_var[:, b, :], moments[:, b, :]).then_inc(gru_v, 1)

            def group(g, par, more):
                candidates(g, par)
                if more:
                    code(g * 2 + (LEAD - 2))
                states(g)
                if more:
                    code(g * 2 + (LEAD - 1))

            LAST = GROUPS - LEAD // 2 + 1
            mix(0)
            candidates(0, 0)
            for c in range(1, NCH):
                mix(c)
            states(0)
            code(3)
            with dve.Fori(0, (LAST - 1) // 2) as it:
                group(it * 2 + 1, 1, True)
                group(it * 2 + 2, 0, True)
            for g in range(LAST, GROUPS):
                group(g, g % 2, False)

            for c in range(1, NCH, 2):
                dve.wait_ge(weights_used, 2 * S - 1 + c // 4)
                dve.tensor_copy(WH[:, chunk(c)], ps[F:P, c // 2, :]).then_inc(wh_out, 1)
            dve.wait_ge(bias_added, 1)
            for q in range(Q):
                dve.wait_ge(projected, q + 1)
                xq = xs[:, q * (S // Q):(q + 1) * (S // Q), :]
                dve.tensor_tensor(xq, ps[:, Q + q, :].rearrange("p (s f) -> p s f", f=F), xq, ALU.add)\
                    .then_inc(final, 1)

        @block.tensor
        def _(pe):
            def mm(dst, lhsT, rhs, start=False, stop=False):
                return pe.matmul(dst, lhsT, rhs, start=start, stop=stop, skip_group_check=True)

            pe.wait_ge(w_loaded, 16 * 4)
            mm(ps[0:F, 7, 0:G], wt_s, win_s, True, True)
            mm(ps[0:F, 7, G:G + 2], wt_s, a2_s, True, True).then_inc(small_w, 1)
            pe.wait_ge(consts, N_CONST)

            def products(it, own_half):
                begin = isinstance(it, int) and it == 0
                for u in range(RING):
                    k, half = divmod(u, 2)
                    if half == 0:
                        pe.wait_ge(staged, it * 10 + (5 * k + 5))
                    first = begin and k == 0
                    pe.wait_ge(masks_made, it * RING + (u + 1))
                    if half == own_half:
                        pe.wait_ge(own_step, it * 4 + (2 * k + 1))
                    for part in range(PARTS):
                        for q in (2 * half, 2 * half + 1):
                            for c in range(2):
                                at = (2 * q + c) * BANK
                                last = mm(ps[c * F:(c + 1) * F, q, :], stage_b[:, k, part * F:(part + 1) * F],
                                          masks[:, at:at + BANK], first and part == 0)
                    last.then_inc(masks_used, 1)
                    pe.wait_ge(tile_loaded[u], it * 16 + 16)
                    if half == own_half:
                        pe.wait_ge(own_step, it * 4 + (2 * k + 2))
                    if first and half == 1:
                        pe.wait_ge(small_w_out, 3)
                    for q in (2 * half, 2 * half + 1):
                        for c in range(2):
                            at = k * N + (2 * q + c) * BANK
                            last = mm(ps[c * F:(c + 1) * F, Q + q, :], stage_f[:, k, :], tiles[:, at:at + BANK], first)
                    last.then_inc(tiles_used, 1)

            products(0, 0)
            with pe.Fori(1, S // 4) as it:
                products(it, 0)
            with pe.Fori(S // 4, S // 2) as it:
                products(it, 1)

            pe.wait_ge(moved_a, 2)
            pe.wait_ge(counts_step, 2 * S)
            for s in range(S):
                last = mm(ps[:, 5, 2 * S + s:2 * S + s + 1], counts[:, s * P:(s + 1) * P], ones[:, 0:1], True, True)
            last.then_inc(degrees, 1)

            def score(c):
                for s in range(c * BC, (c + 1) * BC):
                    last = mm(ps[:, 4, 2 * s:2 * s + 2], X1[0:F, s * P:(s + 1) * P], score_w[0:F, :], True, True)
                return last

            pe.wait_ge(moved_a, 4)
            for c in range(2):
                pe.wait_ge(moved, c + 1)
                score(c)
            pe.wait_ge(flag_step, 4)
            mm(ps[0:1, 5, 0:1], excess[:, 2:3], ones_f[:, :], True, True).then_inc(excess_sum, 1)
            pe.wait_ge(flag_step, 6)
            mm(ps[0:1, 5, 1:2], longest[:, 0:1], ones_f[:, :], True, True).then_inc(excess_sum, 1)
            pe.wait_ge(moved_a, NCH)
            for c in range(NCH):
                if c >= 2:
                    pe.wait_ge(room_ready, c - 1)
                mm(ps[:, 6 + c % 2, :], later[:, :], counts[:, chunk(c)], True, True).then_inc(behind, 1)
                if c >= 2:
                    pe.wait_ge(moved, c + 1)
                    last = score(c)
            last.then_inc(scores, 1)

            def negative_products(s, first):
                pe.wait_ge(neg_v, s * 10 + 11)
                for q in range(Q):
                    for part in range(PARTS):
                        for c in range(2):
                            at = (2 * q + c) * BANK
                            mm(ps[c * F:(c + 1) * F, q, :], stage_b[:, 0, part * F:(part + 1) * F],
                               masks[:, at:at + BANK], first and part == 0)
                    for c in range(2):
                        at = (2 * q + c) * BANK
                        last = mm(ps[c * F:(c + 1) * F, Q + q, :], stage_f[:, 0, :], tiles[:, at:at + BANK], first)
                last.then_inc(neg_used, 1)

            has_neg = load_flag(pe, "pe_neg", 0)
            with pe.If_ne(has_neg, 0):
                pe.wait_ge(room_ready, NCH)
                pe.wait_ge(scores, 1)
                pe.nop().then_inc(neg_used, 1)
                negative_products(0, True)
                with pe.Fori(1, S) as s:
                    negative_products(s, False)
                pe.wait_ge(neg_out, 3 * NCH)
                for s in range(S):
                    mm(ps[:, 0, 2 * s:2 * s + 2], Yn[:, s * P:(s + 1) * P], score_w[F:P, :], True, True)
                    last = mm(ps[:, 0, 2 * S + s:2 * S + s + 1], counts[:, s * P:(s + 1) * P], ones[:, 0:1], True, True)
                last.then_inc(neg_scores, 1)
                pe.wait_ge(neg_out, 3 * NCH + 3)
                for c in range(NCH):
                    last = score(c)
                last.then_inc(neg_scores, 1)

            pe.wait_ge(moved, NCH)
            for c in range(NCH):
                bank, rows = sums_of(c)
                for b in range(BC):
                    last = mm(ps[rows, bank, b * P:(b + 1) * P], h[:, c * BC + b, :], ident[:, :], True, True)
                last.then_inc(turned, 1)

            def spread_weights(w, c, done):
                bank, rows = sums_of(c)
                for b in range(BC):
                    s = c * BC + b
                    last = mm(ps[rows, bank, b * P:(b + 1) * P], w[:, s:s + 1].to_broadcast((P, F)),
                              ident[:, :], True, True)
                last.then_inc(done, 1)

            def mix(c):
                pe.wait_ge(turned_out, c // 2 * 2 + 2)
                spread_weights(pp, c, spread)
                with pe.If_ne(has_neg, 0):
                    pe.wait_ge(mixed, c + 1)
                    spread_weights(pm, c, neg_spread)
                    pe.wait_ge(neg_mixed, 2 * c + 2)

            def cells(g):
                par = g % 2
                if g >= 2:
                    pe.wait_ge(gru_v, (g - 2) * GV + 2)
                for b in range(2):
                    s = 2 * g + b
                    bank = 6 - 2 * par + b
                    mm(ps[:, bank, :], ones[0:PARTS, :], bias_rows[:, :], True)
                    with pe.If_ne(has_neg, 0):
                        mm(ps[:, bank, 0:G], Yn[:, s * P:(s + 1) * P], gate_w[F:P, :]).then_inc(neg_gates, 1)
                        pe.wait_ge(neg_gates, s + 1)
                    mm(ps[:, bank, :], X1[:, s * P:(s + 1) * P], gru_w[:, :])
                    last = mm(ps[:, bank, NODE:HID], Y[:, s * P:(s + 1) * P], gate_w[0:F, :], False, True)
                last.then_inc(gru_pe, 1)

            def decayed(g, odd):
                for half in range(2):
                    pe.wait_ge(weighed, 4 * g + 2 * odd + half + 1)
                    place = weights(g, odd, half)
                    for q in range(2):
                        for part in range(PARTS):
                            for c in range(2):
                                at = (2 * q + c) * BANK
                                last = mm(ps[c * F:(c + 1) * F, 2 * half + q, :],
                                          stage_b[:, 2 * (g % 2) + odd, part * F:(part + 1) * F],
                                          place[:, at:at + BANK].bitcast(BF16), (g, odd, part) == (0, 0, 0))
                    last.then_inc(weights_used, 1)

            pe.wait_ge(bias_moved, 16)
            pe.wait_ge(gru_w_loaded, 16 * 10)
            pe.wait_ge(att_final, 1)
            mix(0)
            pe.wait_ge(mixed, 1)
            cells(0)
            for c in range(1, NCH):
                mix(c)
            cells(1)
            pe.wait_ge(mixed, NCH)
            cells(2)
            for g in range(GROUPS):
                pe.wait_ge(gru_p, GP * (g + 1))
                decayed(g, 0)
                if g + 3 < GROUPS:
                    cells(g + 3)
                decayed(g, 1)
            for q in range(Q):
                pe.wait_ge(wh_out, NCH)
                for b in range(S // Q):
                    s = q * (S // Q) + b
                    last = mm(ps[:, Q + q, b * F:(b + 1) * F], WH[:, s * P:(s + 1) * P], w1_s[:, :], True, True)
                last.then_inc(projected, 1)


_ORDER = ["adj", "adj_diag", "x", "WT", "a2", "wie", "wie_neg", "whe", "win", "whn", "bie", "bhe", "bin", "bhn", "w1", "b1"]


def kernel(**inputs):
    import numpy as _np
    import concourse.bacc as _bacc
    from concourse import mybir as _mybir
    from concourse.bass_utils import run_bass_kernel_spmd as _run

    v = {k: _np.asarray(a) for k, a in inputs.items()}
    L = "L0_gnn_"
    sent = {
        "adj": v["adj"].reshape(P, S, P, S)[:, ::-1, :, ::-1].transpose(2, 3, 1, 0).reshape(P, S * N),
        "adj_diag": v["adj"].diagonal().reshape(P, S)[:, ::-1],
        "x": v["x"].reshape(P, S, F)[:, ::-1],
        "WT": v[L + "W_gat"].T,
        "a2": v[L + "a_gat"].reshape(2, F).T,
        "wie": v[L + "w_ih_e"].T[0:F],
        "wie_neg": v[L + "w_ih_e"].T[F:2 * F],
        "whe": v[L + "w_hh_e"].T,
        "win": v[L + "w_ih_n"].T,
        "whn": v[L + "w_hh_n"].T,
        "bie": v[L + "b_ih_e"],
        "bhe": v[L + "b_hh_e"],
        "bin": v[L + "b_ih_n"],
        "bhn": v[L + "b_hh_n"],
        "w1": v["L1_gnn_weight"],
        "b1": v["L1_gnn_bias"],
    }
    nc = _bacc.Bacc("TRN2", target_bir_lowering=False, num_devices=1)
    arrays, args = {}, []
    for name in _ORDER:
        a = _np.ascontiguousarray(sent[name])
        arrays[f"in_{name}"] = a
        args.append(nc.dram_tensor(f"in_{name}", a.shape, _mybir.dt.from_np(a.dtype), kind="ExternalInput").ap())
    args.append(nc.dram_tensor("out_0", (P, S, F), F32, kind="ExternalOutput").ap())
    graph_layers(nc, *args)
    r = _run(nc, [arrays], core_ids=[0])
    return r.results[0]["out_0"][:, ::-1].reshape(N, F)
```
